# Optimizing a Trainium2 kernel written in Bass

```python
import numpy as np
import jax
import jax.numpy as jnp

def _softmax(x, axis=-1):
    return jax.nn.softmax(x, axis=axis)

def _gelu(x):
    return jax.nn.gelu(x, approximate=True)

def _silu(x):
    return jax.nn.silu(x)

def _sigmoid(x):
    return jax.nn.sigmoid(x)

def _layernorm(x, axis=-1, eps=1e-05):
    m = jnp.mean(x, axis=axis, keepdims=True)
    v = jnp.var(x, axis=axis, keepdims=True)
    return (x - m) / jnp.sqrt(v + eps)

def _scatter_add(tgt, idx, src, axis=0):
    return tgt.at[idx].add(src)

def _segment_sum(src, seg, n):
    return jax.ops.segment_sum(src, seg, n)
kernel_name = 'mk_decoder_postln_d2_seqx_r4_95351d'

def setup_inputs(seed: int=0):
    np.random.seed(seed)
    _w = jnp.asarray

    def _rec_inputs():
        import jax
        import jax.numpy as jnp
        _rk = jax.random.key(seed)
        x = -0.0002928 + 1 * jax.random.normal(jax.random.fold_in(_rk, 1), (8, 256, 512), jnp.float32)
        _lenS = 256 - jax.random.randint(jax.random.fold_in(_rk, 7), (8,), 0, max(1, 256 // 4) + 1, jnp.int32)
        _lenS2 = 256 - jax.random.randint(jax.random.fold_in(_rk, 8), (8,), 0, max(1, 256 // 4) + 1, jnp.int32)
        fside_S2_0 = -0.00337071 + 1.01897 * jax.random.normal(jax.random.fold_in(_rk, 11), (256,), jnp.float32)
        _ctx_2048P = jax.random.normal(jax.random.fold_in(_rk, 12), (8, 16, 512), jnp.float32)
        _ctx_2048c = jax.random.dirichlet(jax.random.fold_in(_rk, 512), 0.3 * jnp.ones((16,), jnp.float32), (8, 256))
        _ctx_2048t = jnp.einsum('bsk,bkd->bsd', _ctx_2048c, _ctx_2048P)
        _ctx_2048t = _ctx_2048t * jax.lax.rsqrt(jnp.mean(jnp.square(_ctx_2048t)) + 1e-12) * 0.953939
        ctx_2048 = 0.000675642 + 1.00031 * (_ctx_2048t + 0.3 * jax.random.normal(jax.random.fold_in(_rk, 612), (8, 256, 512), jnp.float32))
        _validS = jnp.arange(256)[None, :] < _lenS[:, None]
        _validS2 = jnp.arange(256)[None, :] < _lenS2[:, None]
        _causal = jnp.tril(jnp.ones((256, 256), dtype=bool))
        mask_BxSx4224_bf0 = jnp.logical_not(jnp.ones((8, 256, 1056), dtype=bool))
        return (x, fside_S2_0, ctx_2048, mask_BxSx4224_bf0)
    x, fside_S2_0, ctx_2048, mask_BxSx4224_bf0 = _rec_inputs()

    def _L0_attn_setup():
        import math
        import jax, jax.numpy as jnp
        import numpy as np
        EMBED = 512
        NUM_HEADS = 32
        NUM_KV_HEADS = 8
        DEPTH = 12
        H = NUM_HEADS // 2
        KVH = NUM_KV_HEADS // 2
        NREP = H // KVH
        HD = EMBED // NUM_HEADS
        LAMBDA_INIT = 0.8 - 0.6 * math.exp(-0.3 * DEPTH)
        EPS = 1e-05
        B, T = (2, 512)
        key = jax.random.key(seed)
        ks = jax.random.split(key, 10)
        s = 0.02
        return {'x': jax.random.normal(ks[0], (B, T, EMBED), dtype=jnp.float32), 'Wq': jax.random.normal(ks[1], (EMBED, EMBED), dtype=jnp.float32) * s, 'Wk': jax.random.normal(ks[2], (EMBED // NREP, EMBED), dtype=jnp.float32) * s, 'Wv': jax.random.normal(ks[3], (EMBED // NREP, EMBED), dtype=jnp.float32) * s, 'Wo': jax.random.normal(ks[4], (EMBED, EMBED), dtype=jnp.float32) * s, 'lambda_q1': jax.random.normal(ks[5], (HD,), dtype=jnp.float32) * 0.1, 'lambda_k1': jax.random.normal(ks[6], (HD,), dtype=jnp.float32) * 0.1, 'lambda_q2': jax.random.normal(ks[7], (HD,), dtype=jnp.float32) * 0.1, 'lambda_k2': jax.random.normal(ks[8], (HD,), dtype=jnp.float32) * 0.1, 'ln_w': jnp.ones((2 * HD,), dtype=jnp.float32)}
    _L0_attn_all = _L0_attn_setup()
    _L0_attn_in = {k: v for k, v in _L0_attn_all.items() if k in ('Wq', 'Wk', 'Wv', 'Wo', 'lambda_q1', 'lambda_k1', 'lambda_q2', 'lambda_k2', 'ln_w')}
    del _L0_attn_all

    def _L0_xattn_setup():
        import jax, jax.numpy as jnp
        import numpy as np
        key = jax.random.key(seed)
        ks = jax.random.split(key, 5)
        B, D, L, NH = (2, 256, 512, 8)
        H = D // NH
        return {'v': jax.random.normal(ks[0], (B, D, L), jnp.float32), 'k': jax.random.normal(ks[1], (H, L), jnp.float32) * 0.1, 'bias': jax.random.normal(ks[2], (D,), jnp.float32), 'x1': jax.random.normal(ks[3], (B, D, L), jnp.float32), 'x2': jax.random.normal(ks[4], (B, D, L), jnp.float32), 'num_heads': NH}
    _L0_xattn_all = _L0_xattn_setup()
    _L0_xattn_in = {k: v for k, v in _L0_xattn_all.items() if k in ('k',)}
    del _L0_xattn_all

    def _L0_ffn_setup():
        import jax, jax.numpy as jnp
        import numpy as np
        from jax import lax
        TOP_K = 2
        NORM_TOPK = True
        W_SCALE = 0.02
        key = jax.random.key(seed)
        k1, k2, k3, k4 = jax.random.split(key, 4)
        B, S, D = (4, 512, 512)
        E, H = (8, 352)
        x = jax.random.normal(k1, (B, S, D), dtype=jnp.float32)
        gate_up_proj = jax.random.normal(k2, (E, 2 * H, D), dtype=jnp.float32) * W_SCALE
        down_proj = jax.random.normal(k3, (E, D, H), dtype=jnp.float32) * W_SCALE
        router_w = jax.random.normal(k4, (E, D), dtype=jnp.float32) * W_SCALE
        return {'x': x, 'gate_up_proj': gate_up_proj, 'down_proj': down_proj, 'router_w': router_w}
    _L0_ffn_all = _L0_ffn_setup()
    _L0_ffn_in = {k: v for k, v in _L0_ffn_all.items() if k in ('gate_up_proj', 'down_proj', 'router_w')}
    del _L0_ffn_all

    def _L1_attn_setup():
        import jax, jax.numpy as jnp
        import numpy as np
        B, S, D, H = (64, 64, 512, 16)
        HD = D // H
        key = jax.random.key(seed)
        k1, k2, k3 = jax.random.split(key, 3)
        x = jax.random.normal(k1, (B, S, D), dtype=jnp.float32)
        w_qkv = jax.random.normal(k2, (3 * D, D), dtype=jnp.float32) * (1.0 / np.sqrt(D))
        w_o = jax.random.normal(k3, (D, D), dtype=jnp.float32) * (1.0 / np.sqrt(D))
        return {'x': x, 'w_qkv': w_qkv, 'w_o': w_o}
    _L1_attn_all = _L1_attn_setup()
    _L1_attn_in = {k: v for k, v in _L1_attn_all.items() if k in ('w_qkv', 'w_o')}
    del _L1_attn_all

    def _L1_xattn_setup():
        import jax, jax.numpy as jnp
        import numpy as np
        import math
        DIM = 512
        B, Q_LEN, KV_LEN = (8, 128, 1024)
        key = jax.random.key(seed)
        ks = jax.random.split(key, 8)
        x = jax.random.normal(ks[0], (B, Q_LEN, DIM), dtype=jnp.float32)
        mask = jnp.zeros((B, Q_LEN, KV_LEN + Q_LEN), dtype=bool)
        k_cache = jax.random.normal(ks[1], (B, KV_LEN, DIM), dtype=jnp.float32)
        v_cache = jax.random.normal(ks[2], (B, KV_LEN, DIM), dtype=jnp.float32)
        scale = 1.0 / math.sqrt(DIM)
        wq = jax.random.normal(ks[3], (DIM, DIM), dtype=jnp.float32) * scale
        wk = jax.random.normal(ks[4], (DIM, DIM), dtype=jnp.float32) * scale
        wv = jax.random.normal(ks[5], (DIM, DIM), dtype=jnp.float32) * scale
        wo = jax.random.normal(ks[6], (DIM, DIM), dtype=jnp.float32) * scale
        return {'x': x, 'mask': mask, 'k_cache': k_cache, 'v_cache': v_cache, 'wq': wq, 'wk': wk, 'wv': wv, 'wo': wo}
    _L1_xattn_all = _L1_xattn_setup()
    _L1_xattn_in = {k: v for k, v in _L1_xattn_all.items() if k in ('wq', 'wk', 'wv', 'wo')}
    del _L1_xattn_all

    def _L1_ffn_setup():
        import jax, jax.numpy as jnp
        import numpy as np
        import math
        N_EMBD = 512
        N_HEAD = 16
        HEAD_DIM = N_EMBD // N_HEAD
        B, T = (2, 512)
        key = jax.random.key(seed)
        k1, k2, k3 = jax.random.split(key, 3)
        x = jax.random.normal(k1, (B, T, N_EMBD), dtype=jnp.float32)
        W_gate = jax.random.normal(k2, (N_HEAD, N_EMBD), dtype=jnp.float32) * 0.02
        W_qkv = jax.random.normal(k3, (3 * N_EMBD, N_EMBD), dtype=jnp.float32) * 0.02
        return {'x': x, 'W_gate': W_gate, 'W_qkv': W_qkv}
    _L1_ffn_all = _L1_ffn_setup()
    _L1_ffn_in = {k: v for k, v in _L1_ffn_all.items() if k in ('W_gate', 'W_qkv')}
    del _L1_ffn_all
    return {'x': x, 'fside_S2_0': fside_S2_0, 'ctx_2048': ctx_2048, 'mask_BxSx4224_bf0': mask_BxSx4224_bf0, 'L0_attn_Wq': _L0_attn_in['Wq'], 'L0_attn_Wk': _L0_attn_in['Wk'], 'L0_attn_Wv': _L0_attn_in['Wv'], 'L0_attn_Wo': _L0_attn_in['Wo'], 'L0_attn_lambda_q1': _L0_attn_in['lambda_q1'], 'L0_attn_lambda_k1': _L0_attn_in['lambda_k1'], 'L0_attn_lambda_q2': _L0_attn_in['lambda_q2'], 'L0_attn_lambda_k2': _L0_attn_in['lambda_k2'], 'L0_attn_ln_w': _L0_attn_in['ln_w'], 'L0_xattn_k': _L0_xattn_in['k'], 'L0_ffn_gate_up_proj': _L0_ffn_in['gate_up_proj'], 'L0_ffn_down_proj': _L0_ffn_in['down_proj'], 'L0_ffn_router_w': _L0_ffn_in['router_w'], 'L1_attn_w_qkv': _L1_attn_in['w_qkv'], 'L1_attn_w_o': _L1_attn_in['w_o'], 'L1_xattn_wq': _L1_xattn_in['wq'], 'L1_xattn_wk': _L1_xattn_in['wk'], 'L1_xattn_wv': _L1_xattn_in['wv'], 'L1_xattn_wo': _L1_xattn_in['wo'], 'L1_ffn_W_gate': _L1_ffn_in['W_gate'], 'L1_ffn_W_qkv': _L1_ffn_in['W_qkv']}

def reference(x, fside_S2_0, ctx_2048, mask_BxSx4224_bf0, L0_attn_Wq, L0_attn_Wk, L0_attn_Wv, L0_attn_Wo, L0_attn_lambda_q1, L0_attn_lambda_k1, L0_attn_lambda_q2, L0_attn_lambda_k2, L0_attn_ln_w, L0_xattn_k, L0_ffn_gate_up_proj, L0_ffn_down_proj, L0_ffn_router_w, L1_attn_w_qkv, L1_attn_w_o, L1_xattn_wq, L1_xattn_wk, L1_xattn_wv, L1_xattn_wo, L1_ffn_W_gate, L1_ffn_W_qkv):
    import jax
    import jax.numpy as jnp

    def _L0_attn_ref(x, Wq, Wk, Wv, Wo, lambda_q1, lambda_k1, lambda_q2, lambda_k2, ln_w):
        import math
        import jax, jax.numpy as jnp
        import numpy as np
        EMBED = 512
        NUM_HEADS = 32
        NUM_KV_HEADS = 8
        DEPTH = 12
        H = NUM_HEADS // 2
        KVH = NUM_KV_HEADS // 2
        NREP = H // KVH
        HD = EMBED // NUM_HEADS
        LAMBDA_INIT = 0.8 - 0.6 * math.exp(-0.3 * DEPTH)
        EPS = 1e-05
        B, T = (2, 512)
        bsz, tgt, _ = x.shape
        q = (x @ Wq.T).reshape(bsz, tgt, 2 * H, HD)
        k = (x @ Wk.T).reshape(bsz, tgt, 2 * KVH, HD)
        v = (x @ Wv.T).reshape(bsz, tgt, KVH, 2 * HD)
        k = jnp.repeat(k, NREP, axis=2)
        v = jnp.repeat(v, 2 * NREP, axis=2)
        q = q.transpose(0, 2, 1, 3)
        k = k.transpose(0, 2, 1, 3)
        v = v.transpose(0, 2, 1, 3)
        scale = HD ** (-0.5)
        scores = jnp.einsum('bhqd,bhkd->bhqk', q, k) * scale
        causal = jnp.tril(jnp.ones((tgt, tgt), dtype=bool))
        scores = jnp.where(causal, scores, jnp.finfo(scores.dtype).min)
        probs = jax.nn.softmax(scores, axis=-1)
        attn_out = jnp.einsum('bhqk,bhkd->bhqd', probs, v)
        attn1 = attn_out[:, 0::2]
        attn2 = attn_out[:, 1::2]
        lam1 = jnp.exp(jnp.sum(lambda_q1 * lambda_k1))
        lam2 = jnp.exp(jnp.sum(lambda_q2 * lambda_k2))
        lambda_full = lam1 - lam2 + LAMBDA_INIT
        attn = attn1 - lambda_full * attn2
        attn = attn * jax.lax.rsqrt(jnp.mean(attn * attn, axis=-1, keepdims=True) + EPS) * ln_w
        attn = attn * (1.0 - LAMBDA_INIT)
        attn = attn.transpose(0, 2, 1, 3).reshape(bsz, tgt, EMBED)
        return attn @ Wo.T

    def _L0_xattn_ref(v, k, bias, x1, x2, num_heads):
        import jax, jax.numpy as jnp
        import numpy as np
        B, D, L = v.shape
        H = D // num_heads
        fft_size = 2 * L
        vr = v.reshape(B, H, num_heads, L)
        x1r = x1.reshape(B, H, num_heads, L)
        x2r = x2.reshape(B, H, num_heads, L)
        kv = vr[:, :, :, None, :] * x2r[:, :, None, :, :]
        k_f = jnp.fft.rfft(k.astype(jnp.float32), n=fft_size)
        y = jnp.fft.irfft(jnp.fft.rfft(kv, n=fft_size) * k_f[None, :, None, None, :], n=fft_size)[..., :L]
        skip = bias.astype(jnp.float32).reshape(H, num_heads)[None, :, :, None, None]
        y = y + kv * skip
        out = jnp.einsum('bhijl,bhil->bhjl', y, x1r)
        return out.reshape(B, D, L)

    def _L0_ffn_ref(x, gate_up_proj, down_proj, router_w):
        import jax, jax.numpy as jnp
        import numpy as np
        from jax import lax
        TOP_K = 2
        NORM_TOPK = True
        W_SCALE = 0.02
        B, S, D = x.shape
        E = gate_up_proj.shape[0]
        h = x.reshape(-1, D)
        T = h.shape[0]
        logits = h @ router_w.T
        probs = jax.nn.softmax(logits.astype(jnp.float32), axis=-1)
        vals, idx = lax.top_k(probs, TOP_K)
        if NORM_TOPK:
            vals = vals / vals.sum(axis=-1, keepdims=True)
        combine = jnp.zeros((T, E), dtype=probs.dtype)
        combine = combine.at[jnp.arange(T)[:, None], idx].add(vals)

        def step(acc, per_expert):
            gup, dp, cw = per_expert
            gate, up = jnp.split(h @ gup.T, 2, axis=-1)
            y = jax.nn.silu(gate) * up @ dp.T
            return (acc + cw[:, None].astype(acc.dtype) * y, None)
        out, _ = lax.scan(step, jnp.zeros_like(h), (gate_up_proj, down_proj, combine.T))
        return out.reshape(B, S, D)

    def _L1_attn_ref(x, w_qkv, w_o):
        import jax, jax.numpy as jnp
        import numpy as np
        B, S, D, H = (64, 64, 512, 16)
        HD = D // H
        b, s, d = x.shape
        qkv = jnp.einsum('bsd,ed->bse', x, w_qkv)
        qkv = qkv.reshape(b, s, 3, H, HD).transpose(2, 0, 3, 1, 4)
        q, k, v = (qkv[0], qkv[1], qkv[2])
        scores = jnp.einsum('bhqd,bhkd->bhqk', q, k) * HD ** (-0.5)
        causal = jnp.triu(jnp.ones((s, s), dtype=bool), 1)
        scores = jnp.where(causal, jnp.float32(-1000000000.0), scores)
        a = jax.nn.softmax(scores, axis=-1)
        ctx = jnp.einsum('bhqk,bhkd->bhqd', a, v)
        ctx = ctx.transpose(0, 2, 1, 3).reshape(b, s, d)
        return jnp.einsum('bsd,ed->bse', ctx, w_o)

    def _L1_xattn_ref(x, mask, k_cache, v_cache, wq, wk, wv, wo):
        import jax, jax.numpy as jnp
        import numpy as np
        import math
        DIM = 512
        B, Q_LEN, KV_LEN = (8, 128, 1024)
        q = jnp.einsum('bsd,ed->bse', x, wq)
        k_new = jnp.einsum('bsd,ed->bse', x, wk)
        v_new = jnp.einsum('bsd,ed->bse', x, wv)
        k = jnp.concatenate([k_cache, k_new], axis=1)
        v = jnp.concatenate([v_cache, v_new], axis=1)
        scale = 1.0 / math.sqrt(q.shape[-1])
        scores = jnp.einsum('bqd,bkd->bqk', q, k) * scale
        attn = jax.nn.softmax(scores, axis=-1)
        out = jnp.einsum('bqk,bkd->bqd', attn, v)
        return jnp.einsum('bqd,ed->bqe', out, wo)

    def _L1_ffn_ref(x, W_gate, W_qkv):
        import jax, jax.numpy as jnp
        import numpy as np
        import math
        N_EMBD = 512
        N_HEAD = 16
        HEAD_DIM = N_EMBD // N_HEAD
        B, T = (2, 512)
        Bb, Tt, C = x.shape
        H, hd = (N_HEAD, HEAD_DIM)
        gating = jax.nn.softmax(x @ W_gate.T, axis=-1)
        idx = jnp.argmax(gating, axis=-1)
        indicator = jax.nn.one_hot(idx, H, dtype=gating.dtype)
        top1_val = jnp.max(gating, axis=-1, keepdims=True)
        gating_top1 = indicator * top1_val
        qkv = x @ W_qkv.T
        q, k, v = jnp.split(qkv, 3, axis=-1)
        k = k.reshape(Bb, Tt, H, hd)
        v = v.reshape(Bb, Tt, H, hd)
        k_shared = jnp.einsum('bth,bthd->btd', indicator, k)
        v_shared = jnp.einsum('bth,bthd->btd', gating_top1, v)
        q = q.reshape(Bb, Tt, H, hd).transpose(0, 2, 1, 3)
        att = jnp.einsum('bhqd,bkd->bhqk', q, k_shared) * (1.0 / math.sqrt(hd))
        causal = jnp.tril(jnp.ones((Tt, Tt), dtype=bool))
        att = jnp.where(causal[None, None, :, :], att, -jnp.inf)
        att = jax.nn.softmax(att, axis=-1)
        y = jnp.einsum('bhqk,bkd->bhqd', att, v_shared)
        y = y.transpose(0, 2, 1, 3).reshape(Bb, Tt, C)
        return y
    x = _layernorm(x + _L0_attn_ref(x, L0_attn_Wq, L0_attn_Wk, L0_attn_Wv, L0_attn_Wo, L0_attn_lambda_q1, L0_attn_lambda_k1, L0_attn_lambda_q2, L0_attn_lambda_k2, L0_attn_ln_w), axis=-1)
    x = _layernorm(x + _L0_xattn_ref(x, L0_xattn_k, fside_S2_0, ctx_2048, ctx_2048, 8), axis=-1)
    x = _layernorm(x + _L0_ffn_ref(x, L0_ffn_gate_up_proj, L0_ffn_down_proj, L0_ffn_router_w), axis=-1)
    x = _layernorm(x + _L1_attn_ref(x, L1_attn_w_qkv, L1_attn_w_o), axis=-1)
    x = _layernorm(x + _L1_xattn_ref(x, mask_BxSx4224_bf0, ctx_2048, ctx_2048, L1_xattn_wq, L1_xattn_wk, L1_xattn_wv, L1_xattn_wo), axis=-1)
    x = _layernorm(x + _L1_ffn_ref(x, L1_ffn_W_gate, L1_ffn_W_qkv), axis=-1)
    return x

_drawn_inputs = setup_inputs


def setup_inputs(seed=0):
    import zlib

    import numpy as np

    out = dict(_drawn_inputs(seed))
    spreads = {'L0_attn_ln_w': (1.0, 0.543)}
    factors = {'L0_attn_lambda_q1': 8.0,
     'L0_attn_lambda_q2': 7.608,
     'L0_attn_lambda_k2': 5.417,
     'L1_ffn_W_gate': 5.048,
     'L1_ffn_W_qkv': 4.316}
    for name, (base, spread) in spreads.items():
        noise = np.random.default_rng([zlib.crc32(name.encode()), seed]).standard_normal(out[name].shape)
        drawn = base * np.exp(spread * noise) if base else spread * noise
        out[name] = jnp.asarray(drawn.astype(out[name].dtype))
    for name, factor in factors.items():
        out[name] = (out[name] * factor).astype(out[name].dtype)
    return out
```

```python
from contextlib import ExitStack

import math

import concourse.bass as bass
from concourse import mybir

ALU = mybir.AluOpType
ACT = mybir.ActivationFunctionType
AX_X = mybir.AxisListType.X
F32 = mybir.dt.float32
BF16 = mybir.dt.bfloat16

P = 128
B = 8
S = 256
D = 512
NT = S // P
NC = D // P
EPS = 1e-5
MASKED = -1e30
NEVER = -3e38


class Stage:

    def __init__(self, nc, ctx, name):
        self.nc, self.ctx, self.name = nc, ctx, name
        ctx.callback(self.retire)
        self.sems = []

    def sb(self, name, shape, dt=F32):
        return self.ctx.enter_context(self.nc.sbuf_tensor(f"{self.name}_{name}", shape, dt))

    def ps(self, name, shape, dt=F32):
        return self.ctx.enter_context(self.nc.psum_tensor(f"{self.name}_{name}", shape, dt))

    def sem(self, name):
        s = self.nc.alloc_semaphore(f"{self.name}_{name}")
        self.sems.append(s)
        return s

    def retire(self):
        for s in self.sems:
            self.nc.gpsimd.sem_clear(s)
        self.nc.all_engine_barrier()
        for s in self.sems:
            self.nc.release_semaphore(s)


class Link:

    def __init__(self, eng, sem, per):
        self.eng, self.sem, self.per, self.done, self.base = eng, sem, per, 0, 0

    def start(self, b):
        assert self.done in (0, self.per), (self.done, self.per)
        self.base, self.done = b * self.per, 0

    def after(self, ins):
        ins.then_inc(self.sem, 1)
        self.done += 1
        self.eng.wait_ge(self.sem, self.base + self.done)


def make_constants(nc, ctx):
    st = Stage(nc, ctx, "const")
    c = {
        "ident": st.sb("ident", [P, P]),
        "ident_bf": st.sb("ident_bf", [P, P], BF16),
        "mask_bf": st.sb("mask_bf", [P, P], BF16),
        "ones_bf": st.sb("ones_bf", [P, P], BF16),
    }
    c["minus_half"] = st.sb("minus_half", [P, NT * 16])
    c["octets"] = st.sb("octets", [P, P])
    filled, shaped = st.sem("filled"), st.sem("shaped")
    with nc.Block() as block:
        @block.gpsimd
        def _(pool):
            pool.memset(c["ident"][:], 0.0).then_inc(filled, 1)
            pool.memset(c["ident_bf"][:], 0.0).then_inc(filled, 1)
            pool.memset(c["mask_bf"][:], 0.0).then_inc(filled, 1)
            pool.memset(c["ones_bf"][:], 1.0).then_inc(filled, 1)
            pool.memset(c["octets"][:], 1.0).then_inc(filled, 1)
            pool.memset(c["minus_half"][:], -0.5).then_inc(filled, 1)
            pool.wait_ge(filled, 6)
            for name in ("ident", "ident_bf"):
                pool.affine_select(out=c[name][:], in_=c[name][:], compare_op=ALU.not_equal, fill=1.0, base=0,
                                   pattern=[[-1, P]], channel_multiplier=1).then_inc(shaped, 1)
            pool.affine_select(out=c["mask_bf"][:], in_=c["mask_bf"][:], compare_op=ALU.is_ge, fill=MASKED, base=0,
                               pattern=[[-1, P]], channel_multiplier=1).then_inc(shaped, 1)
            octets = c["octets"][:].rearrange("p (a r) -> p a r", r=8)
            pool.affine_select(out=octets, in_=octets, compare_op=ALU.is_ge, fill=0.0, base=0,
                               pattern=[[-8, P // 8], [0, 8]], channel_multiplier=1).then_inc(shaped, 1)
            pool.wait_ge(shaped, 4)
            pool.affine_select(out=octets, in_=octets, compare_op=ALU.is_ge, fill=0.0, base=7,
                               pattern=[[8, P // 8], [0, 8]], channel_multiplier=-1).then_inc(shaped, 1)
            pool.wait_ge(shaped, 5)
    return c



def batches(eng, body):
    with eng.Fori(0, B // 2) as i:
        for p in range(2):
            body(i, p)


class Frame:

    def __init__(self, st, x_in, x_out, extra=None):
        self.st = st
        self.x_in = x_in.rearrange("(b t p) d -> b p t d", p=P, t=NT)
        self.x_out = x_out.rearrange("(b t p) d -> b p t d", p=P, t=NT)
        self.extra = None if extra is None else extra.rearrange("(b t p) d -> b p t d", p=P, t=NT)
        self.x = [st.sb(f"x{p}", [P, NT, D]) for p in range(2)]
        self.normed = [st.sb(f"normed{p}", [P, NT, D]) for p in range(2)]
        self.total = st.sb("total", [P, NT, D])
        self.stats = st.sb("stats", [P, NT, 6])
        self.moments = st.sb("moments", [P, NT, 2])
        self.rstd = st.sb("rstd", [P, NT])
        self.pause = st.sb("pause", [P, 1])
        self.x_loaded = [st.sem(f"x_loaded{p}") for p in range(2)]
        self.stored = [st.sem(f"stored{p}") for p in range(2)]
        self.summed = st.sem("summed")
        self.norm_done = st.sem("norm_done")
        self.var_ready = st.sem("var_ready")
        self.rstd_ready = st.sem("rstd_ready")
        if extra is not None:
            self.e = [st.sb(f"e{p}", [P, NT, D]) for p in range(2)]
            self.e_loaded = [st.sem(f"e_loaded{p}") for p in range(2)]

    def load(self, sp, b, p):
        sp.dma_start(self.x[p][:], self.x_in[b]).then_inc(self.x_loaded[p], 16)
        if self.extra is not None:
            sp.dma_start(self.e[p][:], self.extra[b]).then_inc(self.e_loaded[p], 16)

    def store(self, sp, b, p):
        sp.wait_ge(self.norm_done, b + 1)
        sp.dma_start(self.x_out[b], self.normed[p][:]).then_inc(self.stored[p], 16)

    def traffic(self, sp):
        for p in range(2):
            sp.sem_inc(self.stored[p], 16)
        sp.sem_inc(self.summed, 1)
        for p in range(2):
            self.load(sp, p, p)
        with sp.Fori(0, B // 2 - 1) as i:
            for p in range(2):
                b = 2 * i + p
                sp.wait_ge(self.summed, b + 2)
                self.load(sp, b + 2, p)
                self.store(sp, b, p)
        for p in range(2):
            self.store(sp, B - 2 + p, p)
        for p in range(2):
            sp.wait_ge(self.stored[p], 16 * (B // 2 + 1))

    def root(self, pool, power, b):
        pool.wait_ge(self.var_ready, b + 1)
        pool.tensor_tensor(self.rstd[:], self.rstd[:], power[:, 0:NT], ALU.pow).then_inc(self.rstd_ready, 1)

    LINKS = 2

    def layer_norm(self, dve, link, i, p):
        dve = dve
        for t in range(NT):
            ins = dve.bn_stats(self.stats[:, t, :], self.total[:, t, :])
        link.after(ins)
        dve.memset(self.pause[:], 0.0)
        for t in range(NT):
            ins = dve.bn_aggr(self.moments[:, t, :], self.stats[:, t, :])
        link.after(ins)
        dve.tensor_scalar(self.rstd[:], self.moments[:, :, 1], EPS, None, ALU.add).then_inc(self.var_ready, 1)
        dve.wait_ge(self.stored[p], 16 * i + 16)
        dve.wait_ge(self.rstd_ready, 2 * i + p + 1)
        for t in range(NT):
            ins = dve.tensor_scalar(self.normed[p][:, t, :], self.total[:, t, :], self.moments[:, t, 0:1],
                                     self.rstd[:, t:t + 1], ALU.subtract, ALU.mult)
        ins.then_inc(self.norm_done, 1)


def transpose_rows(pe, ident, out, rows):
    for c in range(NC):
        for t in range(NT):
            ins = pe.transpose(out[:, c // 2, (c % 2) * S + t * P:(c % 2) * S + (t + 1) * P],
                               rows[:, t, c * P:(c + 1) * P], ident[:])
    return ins


def project_cols(pe, out, w, xT, col, n=P):
    for c in range(NC):
        ins = pe.matmul(out, w[:, c, col:col + n], xT[:, c, :], start=c == 0, stop=c == NC - 1)
    return ins


def project_rows(pe, out, xT, t, w, lo, hi):
    for c in range(NC):
        ins = pe.matmul(out, xT[:, c, t * P:(t + 1) * P], w[:, c, lo:hi], start=c == 0, stop=c == NC - 1)
    return ins


class Heads:

    W = P + S

    def __init__(self, st, consts, units, scale, q_of, k_of, v_of, scores, probT_ps, out_ps):
        self.U, self.scale = units, scale
        self.q_of, self.k_of, self.v_of = q_of, k_of, v_of
        self.c = consts
        self.scores, self.probT_ps, self.out_ps = scores, probT_ps, out_ps
        self.probs = st.sb("probs", [P, 2, 2, self.W])
        self.probT = st.sb("probT", [P, 2, self.W])
        self.top = st.sb("top", [P, 2, 2, 2])
        self.shift = st.sb("shift", [P, 2, 2, 2])
        self.sums = st.sb("sums", [P, 4, 2, 2])
        self.inv = st.sb("inv", [P, 4, 2, 2])
        self.scores_ready = st.sem("scores_ready")
        self.shift_ready = st.sem("shift_ready")
        self.probs_ready = st.sem("probs_ready")
        self.probT_ready = st.sem("probT_ready")
        self.copied_act = st.sem("copied_act")
        self.copied_dve = st.sem("copied_dve")
        self.out_ready = st.sem("out_ready")
        self.out_taken = st.sem("out_taken")

    def score(self, pe, b, u):
        if u >= 2:
            pe.wait_ge(self.probs_ready, b * self.U + u - 1)
        for h in range(2):
            bank = self.scores[:, 2 * (u % 2) + h, :]
            for t, kt in ((0, 0), (1, 0), (1, 1)):
                out = bank[:, (t + kt) * P:(t + kt + 1) * P]
                pe.matmul(out, self.q_of(u, h, t), self.k_of(u, h, kt), start=True, stop=t != kt)
                if t == kt:
                    ins = pe.matmul(out, self.c["ident_bf"][:], self.c["mask_bf"][:], start=False, stop=True)
        ins.then_inc(self.scores_ready, 1)

    def turn(self, pe, b, u):
        n = b * self.U + u
        pe.wait_ge(self.probs_ready, n + 1)
        for h in range(2):
            for k in range(3):
                ins = pe.transpose(self.probT_ps[:, h, k * P:(k + 1) * P],
                                   self.probs[:, u % 2, h, k * P:(k + 1) * P], self.c["ident"][:])
        ins.then_inc(self.probT_ready, 1)

    def weigh(self, pe, b, u):
        n = b * self.U + u
        pe.wait_ge(self.copied_act, n + 1)
        pe.wait_ge(self.copied_dve, n + 1)
        if u >= 2:
            pe.wait_ge(self.out_taken, n - 1)
        for h in range(2):
            for t in range(2):
                out = self.out_ps[:, u % 2, t * 64 + h * 32:t * 64 + h * 32 + 32]
                if t == 0:
                    pe.matmul(out, self.probT[:, h, 0:P], self.v_of(u, h, 0), start=True, stop=True)
                else:
                    pe.matmul(out, self.probT[:, h, P:2 * P], self.v_of(u, h, 0), start=True, stop=False)
                    ins = pe.matmul(out, self.probT[:, h, 2 * P:3 * P], self.v_of(u, h, 1), start=False, stop=True)
        ins.then_inc(self.out_ready, 1)

    def tensor(self, pe, b):
        self.score(pe, b, 0)
        for u in range(self.U):
            if u + 1 < self.U:
                self.score(pe, b, u + 1)
            if u >= 1:
                self.weigh(pe, b, u - 1)
            self.turn(pe, b, u)
        self.weigh(pe, b, self.U - 1)

    def exps(self, act, b, u):
        act.wait_ge(self.shift_ready, b * self.U + u + 1)
        if u >= 2:
            act.wait_ge(self.probT_ready, b * self.U + u - 1)
        for h in range(2):
            for t in range(2):
                lo, n = (0, P) if t == 0 else (P, S)
                ins = act.activation(self.probs[:, u % 2, h, lo:lo + n], self.scores[:, 2 * (u % 2) + h, lo:lo + n],
                                     ACT.Exp, bias=self.shift[:, u % 2, t, h:h + 1], scale=self.scale,
                                     accum_out=self.sums[:, u % 4, t, h:h + 1])
        ins.then_inc(self.probs_ready, 1)

    def scalar(self, act, b):
        self.exps(act, b, 0)
        for u in range(self.U):
            act.wait_ge(self.probT_ready, b * self.U + u + 1)
            act.copy(self.probT[:, 0, :], self.probT_ps[:, 0, 0:self.W]).then_inc(self.copied_act, 1)
            if u + 1 < self.U:
                self.exps(act, b, u + 1)

    def maxima(self, dve, link, b, u):
        dve.wait_ge(self.scores_ready, b * self.U + u + 1)
        banks = self.scores[:, 2 * (u % 2):2 * (u % 2) + 2, :]
        dve.tensor_reduce(self.top[:, u % 2, 0, :], banks[:, :, 0:P], AX_X, ALU.max)
        link.after(dve.tensor_reduce(self.top[:, u % 2, 1, :], banks[:, :, P:self.W], AX_X, ALU.max))
        dve.tensor_scalar(self.shift[:, u % 2], self.top[:, u % 2], -self.scale, None,
                          ALU.mult).then_inc(self.shift_ready, 1)

    LINKS_UNIT = 2

    def vector(self, dve, link, b, take):
        self.maxima(dve, link, b, 0)

        def finish(u):
            dve.wait_ge(self.out_ready, b * self.U + u + 1)
            inv = self.inv[:, u % 4]
            link.after(dve.reciprocal(inv, self.sums[:, u % 4]))
            out = self.out_ps[:, u % 2, 0:P].rearrange("p (t h d) -> p t h d", t=2, h=2)
            take(u, out, inv).then_inc(self.out_taken, 1)

        for u in range(self.U):
            if u + 1 < self.U:
                self.maxima(dve, link, b, u + 1)
            dve.wait_ge(self.probT_ready, b * self.U + u + 1)
            dve.tensor_copy(self.probT[:, 1, :], self.probT_ps[:, 1, 0:self.W]).then_inc(self.copied_dve, 1)
            if u >= 1:
                finish(u - 1)
        finish(self.U - 1)


def causal_heads_stage(nc, consts, name, x_in, x_out, w, mode):
    diff, plain, shared = mode == "diff", mode == "plain", mode == "shared"
    with ExitStack() as ctx:
        st = Stage(nc, ctx, name)
        fr = Frame(st, x_in, x_out)
        scores = st.ps("scores", [P, 4, 512])
        probT_ps = st.ps("probT_ps", [P, 2, 512])
        out_ps = st.ps("out_ps", [P, 2, 512])
        gate_ps = out_ps[:, 0, :]
        xT = st.sb("xT", [P, NC, S])
        qT = st.sb("qT", [P, 4, S])
        mixed = st.sb("mixed", [P, NT, D])
        weights_loaded = st.sem("weights_loaded")
        weights_shaped = st.sem("weights_shaped")
        turned_ready = st.sem("turned_ready")
        turned_taken = st.sem("turned_taken")
        proj_ready = st.sem("proj_ready")
        proj_act = st.sem("proj_act")
        proj_dve = st.sem("proj_dve")
        mixed_ready = st.sem("mixed_ready")
        out_proj_ready = st.sem("out_proj_ready")
        linked = st.sem("linked")
        k_turned = st.sem("k_turned")
        k_taken = st.sem("k_taken")
        k_picked = st.sem("k_picked")
        gate_used = st.sem("gate_used")
        gate_exp_in = st.sem("gate_exp_in")
        gate_exp_out = st.sem("gate_exp_out")

        loads = []
        n_loads = len(w)
        wide = {}
        for key, dram in w.items():
            if len(dram.shape) == 2:
                wide[key] = st.sb(key, [P, NC, dram.shape[1]])
                loads.append((wide[key][:], dram.rearrange("(c p) e -> p c e", p=P)))
            else:
                wide[key] = st.sb(key, [P, dram.shape[0]])
                loads.append((wide[key][:], dram.partition_broadcast(P)))

        if diff:
            H2, HD = 32, 16
            kT = st.sb("kT", [P, 8, S])
            v = st.sb("v", [P, NT, P])
            wkz = st.sb("wkz", [P, NC, 4, 2, P])
            pair = st.sb("pair", [P, NT, 2, 32])
            lam = st.sb("lam", [P, 8])
            prod = st.sb("prod", [P, HD])
            square = st.sb("square", [P, NT, D])
            ms = st.sb("ms", [P, NT, 16])
            ms_ready, ms_root = st.sem("ms_ready"), st.sem("ms_root")
            lam_exp_in, lam_exp_out = st.sem("lam_exp_in"), st.sem("lam_exp_out")
            LAMBDA_INIT = 0.8 - 0.6 * math.exp(-0.3 * 12)
            jobs = [("qT", j) for j in range(2)] + [("kT", j) for j in range(4)] + [("v", 0)]
            units = 16
            scale = HD ** -0.5

            def q_of(u, h, t):
                g = u % 4
                return qT[32 * g:32 * g + 32, u // 4, t * P:(t + 1) * P]

            def k_of(u, h, kt):
                g = u % 4
                return kT[32 * g:32 * g + 32, 2 * (u // 4) + h, kt * P:(kt + 1) * P]

            def v_of(u, h, kt):
                return v[:, kt, 32 * (u // 4):32 * (u // 4) + 32]
        else:
            HD = 32
            units = 8
            scale = HD ** -0.5

            def q_of(u, h, t):
                g = (2 * u + h) % 4
                return qT[32 * g:32 * g + 32, u // 2, t * P:(t + 1) * P]
            if plain:
                kT = st.sb("kT", [P, 4, S])
                v = st.sb("v", [P, NT, D])
                jobs = [("qT", 0), ("qT", 1), ("kT", 0), ("kT", 1), ("v", 0), ("v", 1)]

                def k_of(u, h, kt):
                    g = (2 * u + h) % 4
                    return kT[32 * g:32 * g + 32, u // 2, kt * P:(kt + 1) * P]

                def v_of(u, h, kt):
                    return v[:, kt, 32 * (2 * u + h):32 * (2 * u + h) + 32]
            else:
                NG = 16
                kT = st.sb("kT", [P, S])
                v = st.sb("v", [P, NT, 32])
                k4 = st.sb("k4", [P, NT, 4, 32])
                picked = st.sb("picked", [P, 2, D])
                descending = st.sb("descending", [P, NG])
                gl = st.sb("gl", [P, NT, NG])
                gtop = st.sb("gtop", [P, NT])
                gneg = st.sb("gneg", [P, NT])
                ind = st.sb("ind", [P, NT, NG])
                first = st.sb("first", [P, NT])
                gexp = st.sb("gexp", [P, NT, NG])
                gsum = st.sb("gsum", [P, NT])
                gval = st.sb("gval", [P, NT])
                indv = st.sb("indv", [P, NT, NG])
                iota_done = st.sem("iota_done")
                jobs = [("qT", 0), ("qT", 1)]

                def k_of(u, h, kt):
                    g = (2 * u + h) % 4
                    return kT[32 * g:32 * g + 32, kt * P:(kt + 1) * P]

                def v_of(u, h, kt):
                    return v[:, kt, :]

        NJ = len(jobs)
        NJ_ACT, NJ_DVE = (NJ + 1) // 2, NJ // 2
        heads = Heads(st, consts, units, scale, q_of, k_of, v_of, scores, probT_ps, out_ps)
        LINKS = Heads.LINKS_UNIT * units + Frame.LINKS + (2 * units + 3 if diff else 0) + (15 if shared else 0)
        TURNS = 1 if shared else 2

        def job_parts(j):
            kind, n = jobs[j]
            bank = scores[:, j % 4, :]
            if kind == "v":
                return (bank[:, 0:2 * P], v[:].rearrange("p t d -> p (t d)")) if diff else (bank, v[:, n, :])
            dst = {"qT": qT, "kT": kT}[kind]
            return bank, dst[:, 2 * n:2 * n + 2, :].rearrange("p c s -> p (c s)")

        with nc.Block() as block:
            @block.sync
            def _(sp):
                for dst, src in loads:
                    sp.dma_start(dst, src).then_inc(weights_loaded, 16)
                fr.traffic(sp)

            @block.gpsimd
            def _(pool):
                if shared:
                    pool.iota(descending[:], [[-1, NG]], base=NG, channel_multiplier=0,
                              allow_small_or_imprecise_dtypes=True).then_inc(iota_done, 1)

                def batch(i, p):
                    b = 2 * i + p
                    if diff:
                        pool.wait_ge(ms_ready, b + 1)
                        pool.tensor_tensor(ms[:].rearrange("p t h -> p (t h)"), ms[:].rearrange("p t h -> p (t h)"),
                                           consts["minus_half"][:], ALU.pow).then_inc(ms_root, 1)
                    fr.root(pool, consts["minus_half"], b)
                batches(pool, batch)

            @block.tensor
            def _(pe):
                pe.wait_ge(weights_loaded, 16 * n_loads)
                if diff:
                    pe.wait_ge(weights_shaped, 1)

                def batch(i, p):
                    b = 2 * i + p
                    pe.wait_ge(fr.x_loaded[p], 16 * i + 16)
                    transpose_rows(pe, consts["ident"], probT_ps, fr.x[p]).then_inc(turned_ready, 1)
                    pe.wait_ge(turned_taken, TURNS * b + 1)
                    if not shared:
                        pe.wait_ge(fr.summed, b + 1)
                    if shared:
                        for t in range(NT):
                            if t == 1:
                                pe.wait_ge(k_picked, 2 * b + 1)
                            project_rows(pe, gate_ps[:, 0:NG], xT, t, wide["wgate"], 0, NG)
                            project_rows(pe, scores[:, 2, :], xT, t, wide["wk"], 0, D)
                            project_rows(pe, scores[:, 3, :], xT, t, wide["wv"], 0, D).then_inc(gate_used, 1)
                    for j, (kind, n) in enumerate(jobs):
                        if j >= 4:
                            if j % 2:
                                pe.wait_ge(proj_dve, NJ_DVE * b + (j - 4) // 2 + 1)
                            else:
                                pe.wait_ge(proj_act, NJ_ACT * b + (j - 4) // 2 + 1)
                        bank = scores[:, j % 4, :]
                        if kind == "v":
                            if diff:
                                for t in range(NT):
                                    ins = project_rows(pe, bank[:, t * P:(t + 1) * P], xT, t, wide["wv"], 0, P)
                            else:
                                ins = project_rows(pe, bank, xT, n, wide["wv"], 0, D)
                        else:
                            for h in range(2):
                                out = bank[:, h * S:(h + 1) * S]
                                if diff and kind == "kT":
                                    for c in range(NC):
                                        ins = pe.matmul(out, wkz[:, c, n, h, :], xT[:, c, :],
                                                        start=c == 0, stop=c == NC - 1)
                                else:
                                    ins = project_cols(pe, out, wide["w" + kind[0]], xT, (2 * n + h) * P)
                        ins.then_inc(proj_ready, 1)
                    if shared:
                        pe.wait_ge(k_picked, 2 * b + 2)
                        for t in range(NT):
                            ins = pe.transpose(gate_ps[:, P + t * P:P + (t + 1) * P],
                                               k4[:, t].rearrange("p g d -> p (g d)"), consts["ident"][:])
                        ins.then_inc(k_turned, 1)
                        pe.wait_ge(k_taken, b + 1)
                    pe.wait_ge(proj_act, NJ_ACT * (b + 1))
                    pe.wait_ge(proj_dve, NJ_DVE * (b + 1))
                    heads.tensor(pe, b)
                    if shared:
                        pe.wait_ge(heads.out_taken, units * (b + 1))
                    if not shared:
                        pe.wait_ge(mixed_ready, b + 1)
                        transpose_rows(pe, consts["ident"], probT_ps, mixed).then_inc(turned_ready, 1)
                        pe.wait_ge(turned_taken, 2 * b + 2)
                        for t in range(NT):
                            project_rows(pe, scores[:, t, :], xT, t, wide["wo"], 0, D).then_inc(out_proj_ready, 1)

                batches(pe, batch)

            @block.scalar
            def _(act):
                if diff:
                    act.wait_ge(lam_exp_in, 1)
                    act.activation(lam[:, 2:4], lam[:, 0:2], ACT.Exp).then_inc(lam_exp_out, 1)

                def take_turned(b, n):
                    act.wait_ge(turned_ready, TURNS * b + n + 1)
                    act.copy(xT[:].rearrange("p (a c) s -> p a (c s)", a=2), probT_ps[:]).then_inc(turned_taken, 1)

                def batch(i, p):
                    b = 2 * i + p
                    take_turned(b, 0)
                    if shared:
                        act.wait_ge(gate_exp_in, b + 1)
                        act.activation(gexp[:], gl[:], ACT.Exp).then_inc(gate_exp_out, 1)
                    for j in range(0, NJ, 2):
                        src, dst = job_parts(j)
                        act.wait_ge(proj_ready, NJ * b + j + 1)
                        act.copy(dst, src).then_inc(proj_act, 1)
                    if shared:
                        act.wait_ge(k_turned, b + 1)
                        act.copy(kT[:], gate_ps[:, P:P + S]).then_inc(k_taken, 1)
                    heads.scalar(act, b)
                    if not shared:
                        take_turned(b, 1)

                batches(act, batch)

            @block.vector
            def _(dve):
                link = Link(dve, linked, LINKS)
                setup = 0
                if diff or shared:
                    dve.wait_ge(weights_loaded, 16 * n_loads)
                if diff:
                    shaped = st.sem("shaped")
                    setup_link = Link(dve, shaped, 1 << 30)
                    setup_link.after(dve.memset(wkz[:], 0.0))
                    wk = wide["wk"][:].rearrange("p n (c j k) -> p n c j k", c=4, j=2)
                    for s in range(2):
                        for g in range(4):
                            lo = 32 * g + 16 * s
                            ins = dve.tensor_copy(wkz[:, :, :, s, lo:lo + 16], wk[:, :, :, g // 2, :])
                    ins.then_inc(weights_shaped, 1)
                    for n in range(2):
                        setup_link.after(dve.tensor_tensor(prod[:], wide[f"lq{n + 1}"][:], wide[f"lk{n + 1}"][:], ALU.mult))
                        setup_link.after(dve.tensor_reduce(lam[:, n:n + 1], prod[:], AX_X, ALU.add))
                    ins = dve.tensor_scalar(wide["lnw"][:], wide["lnw"][:], 1.0 - LAMBDA_INIT, None, ALU.mult)
                    setup_link.after(ins)
                    dve.nop().then_inc(lam_exp_in, 1)
                    dve.wait_ge(lam_exp_out, 1)
                    setup_link.after(dve.tensor_tensor(lam[:, 4:5], lam[:, 3:4], lam[:, 2:3], ALU.subtract))
                    setup_link.after(dve.tensor_scalar(lam[:, 5:6], lam[:, 4:5], -LAMBDA_INIT, None, ALU.add))
                if shared:
                    dve.wait_ge(iota_done, 1)

                def batch(i, p):
                    b = 2 * i + p
                    link.start(b)
                    if shared:
                        for t in range(NT):
                            dve.wait_ge(gate_used, 2 * b + t + 1)
                            gate = gate_ps[:, 0:NG]
                            link.after(dve.tensor_reduce(gtop[:, t:t + 1], gate, AX_X, ALU.max))
                            dve.tensor_scalar(gl[:, t, :], gate, gtop[:, t:t + 1], None, ALU.subtract)
                            link.after(dve.scalar_tensor_tensor(out=ind[:, t, :], in0=gate, scalar=gtop[:, t:t + 1],
                                                                in1=descending[:], op0=ALU.is_equal, op1=ALU.mult))
                            link.after(dve.tensor_reduce(first[:, t:t + 1], ind[:, t, :], AX_X, ALU.max))
                            link.after(dve.tensor_scalar(ind[:, t, :], ind[:, t, :], first[:, t:t + 1], None, ALU.is_equal))
                            for n, bank in enumerate((2, 3)):
                                ins = dve.tensor_tensor(
                                    picked[:, n, :].rearrange("p (h d) -> p h d", d=HD),
                                    scores[:, bank, :].rearrange("p (h d) -> p h d", d=HD),
                                    ind[:, t, :].unsqueeze(2).to_broadcast([P, NG, HD]), ALU.mult)
                            link.after(ins)
                            dve.tensor_reduce(v[:, t, :], picked[:, 1, :].rearrange("p (h d) -> p d h", d=HD), AX_X, ALU.add)
                            link.after(dve.tensor_reduce(k4[:, t, 0, :], picked[:, 0, :].rearrange("p (h d) -> p d h", d=HD),
                                                         AX_X, ALU.add))
                            dve.tensor_copy(k4[:, t, 1:4, :], k4[:, t, 0:1, :].to_broadcast([P, 3, HD])).then_inc(k_picked, 1)
                        dve.nop().then_inc(gate_exp_in, 1)
                        dve.wait_ge(gate_exp_out, b + 1)
                        link.after(dve.tensor_reduce(gsum[:], gexp[:], AX_X, ALU.add))
                        link.after(dve.reciprocal(gval[:], gsum[:]))
                        for t in range(NT):
                            ins = dve.tensor_scalar(v[:, t, :], v[:, t, :], gval[:, t:t + 1], None, ALU.mult)
                        link.after(ins)
                    for j in range(1, NJ, 2):
                        src, dst = job_parts(j)
                        dve.wait_ge(proj_ready, NJ * b + j + 1)
                        dve.tensor_copy(dst, src).then_inc(proj_dve, 1)

                    if diff:
                        def take(u, out, inv):
                            a1 = mixed[:, :, 32 * u:32 * u + 32]
                            link.after(dve.tensor_scalar(inv[:, :, 1], inv[:, :, 1], lam[:, 5:6], None, ALU.mult))
                            link.after(dve.tensor_tensor(pair[:], out, inv.unsqueeze(3).to_broadcast([P, 2, 2, 32]), ALU.mult))
                            return dve.tensor_tensor(a1, pair[:, :, 0, :], pair[:, :, 1, :], ALU.add)
                    else:
                        target = mixed

                        def take(u, out, inv):
                            dst = target[:, :, 64 * u:64 * u + 64].rearrange("p t (h d) -> p t h d", h=2)
                            return dve.tensor_tensor(dst, out, inv.unsqueeze(3).to_broadcast([P, 2, 2, 32]), ALU.mult)

                    heads.vector(dve, link, b, take)
                    dve.wait_ge(heads.out_taken, units * (b + 1))
                    if diff:
                        m4 = mixed[:].rearrange("p t (h d) -> p t h d", d=32)
                        link.after(dve.tensor_tensor(square[:], mixed[:], mixed[:], ALU.mult))
                        link.after(dve.tensor_reduce(ms[:], square[:].rearrange("p t (h d) -> p t h d", d=32), AX_X, ALU.add))
                        dve.tensor_scalar(ms[:], ms[:], 1.0 / 32, EPS, ALU.mult, ALU.add).then_inc(ms_ready, 1)
                        dve.wait_ge(ms_root, b + 1)
                        for t in range(NT):
                            ins = dve.tensor_tensor(m4[:, t], m4[:, t], ms[:, t].unsqueeze(2).to_broadcast([P, 16, 32]), ALU.mult)
                        link.after(ins)
                        for t in range(NT):
                            ins = dve.tensor_tensor(m4[:, t], m4[:, t], wide["lnw"][:].unsqueeze(1).to_broadcast([P, 16, 32]), ALU.mult)
                    if not shared:
                        dve.nop().then_inc(mixed_ready, 1) if plain else ins.then_inc(mixed_ready, 1)
                        for t in range(NT):
                            dve.wait_ge(out_proj_ready, 2 * b + t + 1)
                            ins = dve.tensor_tensor(fr.total[:, t, :], scores[:, t, :], fr.x[p][:, t, :], ALU.add)
                    else:
                        dve.wait_ge(fr.x_loaded[p], 16 * i + 16)
                        ins = dve.tensor_tensor(fr.total[:], mixed[:], fr.x[p][:], ALU.add)
                    ins.then_inc(fr.summed, 1)
                    dve.wait_ge(fr.summed, b + 2)
                    fr.layer_norm(dve, link, i, p)

                batches(dve, batch)



def long_conv_stage(nc, consts, name, x_in, x_out, ctx_in, toeplitz, toep_stored, skip):
    H, NI = 32, 8
    with ExitStack() as ctx:
        st = Stage(nc, ctx, name)
        vT = st.sb("vT", [P, NC, B, S])
        cT = st.sb("cT", [P, NC, B, S])

        with ExitStack() as ctx_a:
            sa = Stage(nc, ctx_a, name + "A")
            src = [[sa.sb(f"src{p}{n}", [P, NT, D]) for n in range(2)] for p in range(2)]
            ps = [sa.ps(f"ps{n}", [P, 2, 512]) for n in range(2)]
            loaded = [[sa.sem(f"loaded{p}{n}") for n in range(2)] for p in range(2)]
            turned = [sa.sem(f"turned{n}") for n in range(2)]
            taken = [sa.sem(f"taken{n}") for n in range(2)]
            rows = [a.rearrange("(b t p) d -> b p t d", p=P, t=NT) for a in (x_in, ctx_in)]
            with nc.Block() as block:
                @block.sync
                def _(sp):
                    for p in range(2):
                        for n in range(2):
                            sp.dma_start(src[p][n][:], rows[n][p]).then_inc(loaded[p][n], 16)
                    with sp.Fori(0, B // 2 - 1) as i:
                        for p in range(2):
                            for n in range(2):
                                sp.wait_ge(turned[n], 2 * i + p + 1)
                                sp.dma_start(src[p][n][:], rows[n][2 * i + p + 2]).then_inc(loaded[p][n], 16)

                @block.tensor
                def _(pe):
                    for n in range(2):
                        pe.sem_inc(taken[n], 1)

                    def batch(i, p):
                        for n in range(2):
                            pe.wait_ge(loaded[p][n], 16 * i + 16)
                            pe.wait_ge(taken[n], 2 * i + p + 1)
                            transpose_rows(pe, consts["ident"], ps[n], src[p][n]).then_inc(turned[n], 1)
                    batches(pe, batch)

                @block.scalar
                def _(act):
                    def batch(i, p):
                        act.wait_ge(turned[0], 2 * i + p + 1)
                        act.copy(vT[:, :, 2 * i + p, :],
                                 ps[0][:].rearrange("p a (c s) -> p (a c) s", c=2)).then_inc(taken[0], 1)
                    batches(act, batch)

                @block.vector
                def _(dve):
                    def batch(i, p):
                        dve.wait_ge(turned[1], 2 * i + p + 1)
                        dve.tensor_copy(cT[:, :, 2 * i + p, :],
                                        ps[1][:].rearrange("p a (c s) -> p (a c) s", c=2)).then_inc(taken[1], 1)
                    batches(dve, batch)

        with ExitStack() as ctx_b:
            sb_ = Stage(nc, ctx_b, name + "B")
            toep = [sb_.sb(f"toep{p}", [P, D]) for p in range(2)]
            kv = [sb_.sb(f"kv{p}", [P, NC, B, NI, NI]) for p in range(2)]
            prod = sb_.sb("prod", [P, 2, B, NI, NI])
            conv = sb_.ps("conv", [P, 8, 512])
            toep_loaded = [sb_.sem(f"toep_loaded{p}") for p in range(2)]
            kv_ready = sb_.sem("kv_ready")
            conv_ready = sb_.sem("conv_ready")
            prod_ready = sb_.sem("prod_ready")

            def pairs_of(buf, c, h, over):
                a = buf[:, c, :, bass.ds(h * NI, NI)]
                return a.unsqueeze(3 if over == "i" else 2).to_broadcast([P, B, NI, NI])

            def heads_loop(eng, body):
                for p in range(2):
                    body(p, p, False)
                with eng.Fori(1, H // 2) as i:
                    for p in range(2):
                        body(2 * i + p, p, True)

            with nc.Block() as block:
                @block.sync
                def _(sp):
                    sp.wait_ge(toep_stored, 16)

                    def head(h, p, steady):
                        if steady:
                            sp.wait_ge(conv_ready, NC * h - NC)
                        sp.dma_start(toep[p][:], toeplitz[h]).then_inc(toep_loaded[p], 16)
                    heads_loop(sp, head)

                @block.gpsimd
                def _(pool):
                    def head(h, p, steady):
                        if steady:
                            pool.wait_ge(conv_ready, NC * h - NC)
                        for c in range(NC):
                            pool.tensor_tensor(kv[p][:, c], pairs_of(vT, c, h, "i"), pairs_of(cT, c, h, "j"),
                                               ALU.mult).then_inc(kv_ready, 1)
                    heads_loop(pool, head)

                @block.tensor
                def _(pe):
                    def head(h, p, steady):
                        pe.wait_ge(toep_loaded[p], h * 8 + 16 - 8 * p)
                        for lc in range(NC):
                            pe.wait_ge(kv_ready, NC * h + lc + 1)
                            if steady:
                                pe.wait_ge(prod_ready, NC * h + lc + 1 - 2 * NC)
                            for c in range(lc + 1):
                                lo = (lc - c) * P
                                ins = pe.matmul(conv[:, NC * p + lc, :], toep[p][:, lo:lo + P],
                                                kv[p][:, c].rearrange("p b i j -> p (b i j)"),
                                                start=c == 0, stop=c == lc)
                            ins.then_inc(conv_ready, 1)
                    heads_loop(pe, head)

                @block.vector
                def _(dve):
                    def head(h, p, steady):
                        for lc in range(NC):
                            dve.wait_ge(conv_ready, NC * h + lc + 1)
                            bank = conv[:, NC * p + lc, :].rearrange("p (b i j) -> p b i j", i=NI, j=NI)
                            dve.tensor_tensor(prod[:, lc % 2], bank, pairs_of(cT, lc, h, "i"),
                                              ALU.mult).then_inc(prod_ready, 1)
                            dve.wait_ge(prod_ready, NC * h + lc + 1)
                            dve.tensor_reduce(vT[:, lc, :, bass.ds(h * NI, NI)],
                                              prod[:, lc % 2].rearrange("p b i j -> p b j i"), AX_X, ALU.add)
                    heads_loop(dve, head)

        with ExitStack() as ctx_c:
            sc = Stage(nc, ctx_c, name + "C")
            fr = Frame(sc, x_in, x_out, ctx_in)
            skips = sc.sb("skips", [P, NT])
            skipped = sc.sb("skipped", [P, NT, D])
            part = sc.sb("part", [P, NT, D])
            result = sc.sb("result", [P, NC, S])
            back = [sc.ps(f"back{p}", [P, NT, 512]) for p in range(2)]
            osum = [sc.ps(f"osum{p}", [P, NT, 512]) for p in range(2)]
            skip_loaded = sc.sem("skip_loaded")
            result_copied, skipped_ready = sc.sem("result_copied"), sc.sem("skipped_ready")
            back_ready, osum_ready, linked = sc.sem("back_ready"), sc.sem("osum_ready"), sc.sem("linked")
            with nc.Block() as block:
                @block.sync
                def _(sp):
                    sp.dma_start(skips[:], skip.rearrange("(t p) -> p t", p=P), allow_slow_non_contiguous=True).then_inc(skip_loaded, 16)
                    fr.traffic(sp)

                @block.gpsimd
                def _(pool):
                    batches(pool, lambda i, p: fr.root(pool, consts["minus_half"], 2 * i + p))

                @block.scalar
                def _(act):
                    act.sem_inc(back_ready, 1)

                    def batch(i, p):
                        b = 2 * i + p
                        act.wait_ge(back_ready, b + 1)
                        act.copy(result[:], vT[:, :, b, :]).then_inc(result_copied, 1)
                    batches(act, batch)

                @block.tensor
                def _(pe):
                    def batch(i, p):
                        b = 2 * i + p
                        pe.wait_ge(result_copied, b + 1)
                        pe.wait_ge(fr.summed, b + 1)
                        for t in range(NT):
                            for c in range(NC):
                                ins = pe.transpose(back[p][:, t, c * P:(c + 1) * P], result[:, c, t * P:(t + 1) * P],
                                                   consts["ident"][:])
                        ins.then_inc(back_ready, 1)
                        pe.wait_ge(skipped_ready, b + 1)
                        for t in range(NT):
                            ins = pe.matmul(osum[p][:, t, :], consts["octets"][:], skipped[:, t, :], start=True, stop=True)
                        ins.then_inc(osum_ready, 1)
                    batches(pe, batch)

                @block.vector
                def _(dve):
                    link = Link(dve, linked, Frame.LINKS + 1)
                    dve.wait_ge(skip_loaded, 16)

                    def batch(i, p):
                        b = 2 * i + p
                        link.start(b)
                        dve.wait_ge(fr.x_loaded[p], 16 * i + 16)
                        dve.wait_ge(fr.e_loaded[p], 16 * i + 16)
                        for t in range(NT):
                            ins = dve.scalar_tensor_tensor(out=skipped[:, t, :], in0=fr.x[p][:, t, :], scalar=skips[:, t:t + 1],
                                                           in1=fr.e[p][:, t, :], op0=ALU.mult, op1=ALU.mult)
                        ins.then_inc(skipped_ready, 1)
                        dve.wait_ge(back_ready, b + 2)
                        dve.tensor_tensor(part[:], back[p][:], fr.x[p][:], ALU.add)
                        dve.wait_ge(osum_ready, b + 1)
                        link.after(dve.tensor_tensor(fr.total[:], osum[p][:], fr.e[p][:], ALU.mult))
                        dve.tensor_tensor(fr.total[:], fr.total[:], part[:], ALU.add).then_inc(fr.summed, 1)
                        dve.wait_ge(fr.summed, b + 2)
                        fr.layer_norm(dve, link, i, p)
                    batches(dve, batch)


def long_cross_stage(nc, consts, name, x_in, x_out, ctx_in, w):
    KT = 2 * NT
    SCALE = 1.0 / math.sqrt(D)
    with ExitStack() as ctx:
        st = Stage(nc, ctx, name)
        fr = Frame(st, x_in, x_out, ctx_in)
        banks = st.ps("banks", [P, 4, 512])
        turn_ps = st.ps("turn_ps", [P, 2, 2, 512])
        xT = st.sb("xT", [P, NC, S])
        qT = st.sb("qT", [P, NC, S])
        kT = st.sb("kT", [P, NC, 2 * S])
        v = st.sb("v", [P, NT, D])
        probs = st.sb("probs", [P, NT, 2 * S])
        probT = st.sb("probT", [P, NT, KT, P])
        mixed = st.sb("mixed", [P, NT, D])
        top, shift, sums, inv = (st.sb(n, [P, NT]) for n in ("top", "shift", "sums", "inv"))
        wide = {k: st.sb(k, [P, NC, D]) for k in w}
        sem = {n: st.sem(n) for n in (
            "weights_loaded", "x_turned", "x_taken", "e_turned", "e_taken", "proj_ready", "proj_act", "proj_dve",
            "scores_ready", "shift_ready", "probs_ready", "probs_turned", "probT_act", "probT_dve", "mixed_raw",
            "mixed_ready", "mixed_turned", "mixed_taken", "out_ready", "linked")}
        LINKS = Frame.LINKS + 3
        with nc.Block() as block:
            @block.sync
            def _(sp):
                for k in w:
                    sp.dma_start(wide[k][:], w[k].rearrange("(c p) e -> p c e", p=P)).then_inc(sem["weights_loaded"], 16)
                fr.traffic(sp)

            @block.tensor
            def _(pe):
                pe.wait_ge(sem["weights_loaded"], 16 * len(w))

                def batch(i, p):
                    b = 2 * i + p
                    pe.wait_ge(fr.x_loaded[p], 16 * i + 16)
                    transpose_rows(pe, consts["ident"], turn_ps[:, 0], fr.x[p]).then_inc(sem["x_turned"], 1)
                    pe.wait_ge(fr.e_loaded[p], 16 * i + 16)
                    transpose_rows(pe, consts["ident"], turn_ps[:, 1], fr.e[p]).then_inc(sem["e_turned"], 1)
                    pe.wait_ge(sem["x_taken"], b + 1)
                    pe.wait_ge(fr.summed, b + 1)
                    for j in range(4):
                        for h in range(2):
                            ins = project_cols(pe, banks[:, j, h * S:(h + 1) * S], wide["wq" if j < 2 else "wk"], xT,
                                               (2 * (j % 2) + h) * P)
                        ins.then_inc(sem["proj_ready"], 1)
                    for t in range(NT):
                        pe.wait_ge(sem["proj_dve"] if t else sem["proj_act"], 3 * b + 1)
                        project_rows(pe, banks[:, t, :], xT, t, wide["wv"], 0, D).then_inc(sem["proj_ready"], 1)
                    pe.wait_ge(sem["e_taken"], b + 1)
                    pe.wait_ge(sem["proj_act"], 3 * b + 2)
                    pe.wait_ge(sem["proj_dve"], 3 * b + 2)
                    for t in range(NT):
                        for c in range(NC):
                            ins = pe.matmul(banks[:, 2 + t, :], qT[:, c, t * P:(t + 1) * P], kT[:, c, :],
                                            start=c == 0, stop=c == NC - 1)
                        ins.then_inc(sem["scores_ready"], 1)
                    for t in range(NT):
                        pe.wait_ge(sem["probs_ready"], 2 * b + t + 1)
                        for k in range(KT):
                            ins = pe.transpose(turn_ps[:, 0, t, k * P:(k + 1) * P], probs[:, t, k * P:(k + 1) * P],
                                               consts["ident"][:])
                        ins.then_inc(sem["probs_turned"], 1)
                    pe.wait_ge(sem["proj_act"], 3 * b + 3)
                    pe.wait_ge(sem["proj_dve"], 3 * b + 3)
                    for t in range(NT):
                        pe.wait_ge(sem["probT_dve"] if t else sem["probT_act"], b + 1)
                        for k in range(KT):
                            val = fr.e[p][:, k, :] if k < NT else v[:, k - NT, :]
                            ins = pe.matmul(banks[:, t, :], probT[:, t, k, :], val, start=k == 0, stop=k == KT - 1)
                        ins.then_inc(sem["mixed_raw"], 1)
                    pe.wait_ge(sem["mixed_ready"], b + 1)
                    transpose_rows(pe, consts["ident"], turn_ps[:, 1], mixed).then_inc(sem["mixed_turned"], 1)
                    pe.wait_ge(sem["mixed_taken"], b + 1)
                    for t in range(NT):
                        project_rows(pe, banks[:, 2 + t, :], xT, t, wide["wo"], 0, D).then_inc(sem["out_ready"], 1)

                batches(pe, batch)

            def turned(half, dst):
                return dst.rearrange("p (a c) s -> p a c s", a=2), turn_ps[:, half].rearrange("p a (c s) -> p a c s", c=2)

            @block.gpsimd
            def _(pool):
                batches(pool, lambda i, p: fr.root(pool, consts["minus_half"], 2 * i + p))

            @block.scalar
            def _(act):
                def batch(i, p):
                    b = 2 * i + p
                    act.wait_ge(sem["x_turned"], b + 1)
                    act.copy(*turned(0, xT[:])).then_inc(sem["x_taken"], 1)
                    for n, dst in enumerate((qT[:, 0:2, :], kT[:, 0:2, S:2 * S], None)):
                        act.wait_ge(sem["proj_ready"], 6 * b + 2 * n + 1)
                        if n < 2:
                            act.copy(dst, banks[:, 2 * n, :].rearrange("p (c s) -> p c s", c=2)).then_inc(sem["proj_act"], 1)
                        else:
                            act.copy(v[:, 0, :], banks[:, 0, :]).then_inc(sem["proj_act"], 1)
                    for t in range(NT):
                        act.wait_ge(sem["shift_ready"], 2 * b + t + 1)
                        act.activation(probs[:, t, :], banks[:, 2 + t, :], ACT.Exp, bias=shift[:, t:t + 1], scale=SCALE,
                                       accum_out=sums[:, t:t + 1]).then_inc(sem["probs_ready"], 1)
                    act.wait_ge(sem["probs_turned"], 2 * b + 1)
                    act.copy(probT[:, 0].rearrange("p k q -> p (k q)"), turn_ps[:, 0, 0, :]).then_inc(sem["probT_act"], 1)
                    act.wait_ge(sem["mixed_turned"], b + 1)
                    act.copy(*turned(1, xT[:])).then_inc(sem["mixed_taken"], 1)

                batches(act, batch)

            @block.vector
            def _(dve):
                link = Link(dve, sem["linked"], LINKS)

                def batch(i, p):
                    b = 2 * i + p
                    link.start(b)
                    dve.wait_ge(sem["e_turned"], b + 1)
                    dst, src = turned(1, kT[:, :, 0:S])
                    for a in range(2):
                        ins = dve.tensor_copy(dst[:, a], src[:, a])
                    ins.then_inc(sem["e_taken"], 1)
                    for n, dst in enumerate((qT[:, 2:4, :], kT[:, 2:4, S:2 * S], None)):
                        dve.wait_ge(sem["proj_ready"], 6 * b + 2 * n + 2)
                        if n < 2:
                            dve.tensor_copy(dst, banks[:, 2 * n + 1, :].rearrange("p (c s) -> p c s", c=2)).then_inc(sem["proj_dve"], 1)
                        else:
                            dve.tensor_copy(v[:, 1, :], banks[:, 1, :]).then_inc(sem["proj_dve"], 1)
                    for t in range(NT):
                        dve.wait_ge(sem["scores_ready"], 2 * b + t + 1)
                        link.after(dve.tensor_reduce(top[:, t:t + 1], banks[:, 2 + t, :], AX_X, ALU.max))
                        dve.tensor_scalar(shift[:, t:t + 1], top[:, t:t + 1], -SCALE, None, ALU.mult).then_inc(sem["shift_ready"], 1)
                    dve.wait_ge(sem["probs_turned"], 2 * b + 2)
                    dve.tensor_copy(probT[:, 1].rearrange("p k q -> p (k q)"), turn_ps[:, 0, 1, :]).then_inc(sem["probT_dve"], 1)
                    link.after(dve.reciprocal(inv[:], sums[:]))
                    for t in range(NT):
                        dve.wait_ge(sem["mixed_raw"], 2 * b + t + 1)
                        ins = dve.tensor_scalar(mixed[:, t, :], banks[:, t, :], inv[:, t:t + 1], None, ALU.mult)
                    ins.then_inc(sem["mixed_ready"], 1)
                    for t in range(NT):
                        dve.wait_ge(sem["out_ready"], 2 * b + t + 1)
                        ins = dve.tensor_tensor(fr.total[:, t, :], banks[:, 2 + t, :], fr.x[p][:, t, :], ALU.add)
                    ins.then_inc(fr.summed, 1)
                    dve.wait_ge(fr.summed, b + 2)
                    fr.layer_norm(dve, link, i, p)

                batches(dve, batch)


def experts_stage(nc, consts, name, x_in, x_out, w_router, w_gu, w_down):
    E, HID = 8, 352
    HC = [(0, P), (P, P), (2 * P, HID - 2 * P)]
    with ExitStack() as ctx:
        st = Stage(nc, ctx, name)
        fr = Frame(st, x_in, x_out)
        gu_ps = st.ps("gu_ps", [P, NT, 2, 512])
        hT_ps = st.ps("hT_ps", [P, NT, 512])
        y_ps = st.ps("y_ps", [P, NT, 512])
        wr = st.sb("wr", [P, NC, E])
        wgu = st.sb("wgu", [P, E, NC, 2 * HID])
        wd = st.sb("wd", [P, E, 3, D])
        xT = st.sb("xT", [P, NC, S])
        silu = st.sb("silu", [P, NT, HID])
        hid = st.sb("hid", [P, NT, HID])
        hT = st.sb("hT", [P, NT, 3, P])
        desc = st.sb("desc", [P, E])
        lg = st.sb("lg", [P, NT, E])
        rank = st.sb("rank", [P, NT, E])
        top = st.sb("top", [P, NT, 2])
        which = st.sb("which", [P, NT, 2])
        ind = st.sb("ind", [P, NT, 2, E])
        diffs = st.sb("diffs", [P, NT])
        share = st.sb("share", [P, NT, 2])
        den = st.sb("den", [P, NT])
        cw = st.sb("cw", [P, NT, E])
        sem = {n: st.sem(n) for n in (
            "weights_loaded", "desc_done", "x_turned", "x_taken", "logits_ready", "diff_ready", "exp_ready", "gu_ready",
            "loop_pe", "loop_act", "loop_dve", "silu_ready", "hid_ready", "h_turned", "hT_taken", "y_ready", "y_used", "linked")}
        LINKS = Frame.LINKS + 16
        with nc.Block() as block:
            @block.sync
            def _(sp):
                sp.dma_start(wr[:], w_router.rearrange("(c p) e -> p c e", p=P)).then_inc(sem["weights_loaded"], 16)
                for e in range(E):
                    sp.dma_start(wgu[:, e], w_gu[e].rearrange("(c p) n -> p c n", p=P)).then_inc(sem["weights_loaded"], 16)
                    sp.dma_start(wd[:, e, 0:2, :], w_down[e, 0:2 * P].rearrange("(c p) n -> p c n", p=P)).then_inc(sem["weights_loaded"], 16)
                    sp.dma_start(wd[0:HID - 2 * P, e, 2, :], w_down[e, 2 * P:HID]).then_inc(sem["weights_loaded"], 16)
                fr.traffic(sp)

            @block.gpsimd
            def _(pool):
                pool.iota(desc[:], [[-1, E]], base=E, channel_multiplier=0,
                          allow_small_or_imprecise_dtypes=True).then_inc(sem["desc_done"], 1)
                batches(pool, lambda i, p: fr.root(pool, consts["minus_half"], 2 * i + p))

            @block.tensor
            def _(pe):
                pe.wait_ge(sem["weights_loaded"], 16 * (1 + 3 * E))

                def batch(i, p):
                    b = 2 * i + p
                    pe.wait_ge(fr.x_loaded[p], 16 * i + 16)
                    transpose_rows(pe, consts["ident"], hT_ps, fr.x[p]).then_inc(sem["x_turned"], 1)
                    pe.wait_ge(sem["x_taken"], b + 1)
                    pe.wait_ge(sem["y_used"], 2 * E * b + 2)
                    for t in range(NT):
                        ins = project_rows(pe, y_ps[:, t, 0:E], xT, t, wr, 0, E)
                    ins.then_inc(sem["logits_ready"], 1)
                    pe.wait_ge(sem["diff_ready"], b + 1)
                    pe.sem_inc(sem["loop_pe"], 1)
                    with pe.Fori(0, E) as e:
                        n = (b * E + e) * 2
                        for t in range(NT):
                            pe.wait_ge(sem["hid_ready"], n + 1)
                            for h in range(2):
                                for c in range(NC):
                                    ins = pe.matmul(gu_ps[:, t, h, 0:HID], xT[:, c, t * P:(t + 1) * P],
                                                    wgu[:, e, c, h * HID:(h + 1) * HID],
                                                    start=c == 0, stop=c == NC - 1)
                            ins.then_inc(sem["gu_ready"], 1)
                        for t in range(NT):
                            pe.wait_ge(sem["hid_ready"], n + t + 2)
                            for k, (lo, m) in enumerate(HC):
                                ins = pe.transpose(hT_ps[0:m, t, k * P:(k + 1) * P], hid[:, t, lo:lo + m], consts["ident"][:])
                            ins.then_inc(sem["h_turned"], 1)
                        for t in range(NT):
                            pe.wait_ge(sem["hT_taken"], n + t + 1)
                            pe.wait_ge(sem["y_used"], n + 2)
                            for k, (lo, m) in enumerate(HC):
                                ins = pe.matmul(y_ps[:, t, :], hT[0:m, t, k, :], wd[0:m, e, k, :], start=k == 0, stop=k == 2)
                            ins.then_inc(sem["y_ready"], 1)

                batches(pe, batch)

            @block.scalar
            def _(act):
                def batch(i, p):
                    b = 2 * i + p
                    act.wait_ge(sem["x_turned"], b + 1)
                    act.copy(xT[:].rearrange("p (a c) s -> p a (c s)", a=2), hT_ps[:]).then_inc(sem["x_taken"], 1)
                    act.wait_ge(sem["diff_ready"], b + 1)
                    act.activation(share[:, :, 1], diffs[:], ACT.Exp).then_inc(sem["exp_ready"], 1)
                    act.sem_inc(sem["loop_act"], 1)
                    with act.Fori(0, E) as e:
                        n = (b * E + e) * 2
                        for t in range(NT):
                            act.wait_ge(sem["gu_ready"], n + t + 1)
                            act.activation(silu[:, t, :], gu_ps[:, t, 0, 0:HID], ACT.Silu).then_inc(sem["silu_ready"], 1)
                        for t in range(NT):
                            act.wait_ge(sem["h_turned"], n + t + 1)
                            act.copy(hT[:, t, 0:2].rearrange("p k q -> p (k q)"), hT_ps[:, t, 0:2 * P])
                            m = HC[2][1]
                            act.copy(hT[0:m, t, 2], hT_ps[0:m, t, 2 * P:3 * P]).then_inc(sem["hT_taken"], 1)

                batches(act, batch)

            @block.vector
            def _(dve):
                link = Link(dve, sem["linked"], LINKS)
                dve.wait_ge(sem["desc_done"], 1)
                dve.sem_inc(sem["hid_ready"], 1)
                dve.sem_inc(sem["y_used"], 2)

                def batch(i, p):
                    b = 2 * i + p
                    link.start(b)
                    dve.wait_ge(sem["logits_ready"], b + 1)
                    link.after(dve.tensor_copy(lg[:], y_ps[:, :, 0:E]))
                    for n in range(2):
                        link.after(dve.tensor_reduce(top[:, :, n], lg[:], AX_X, ALU.max))
                        for t in range(NT):
                            ins = dve.scalar_tensor_tensor(out=rank[:, t, :], in0=lg[:, t, :], scalar=top[:, t, n:n + 1],
                                                           in1=desc[:], op0=ALU.is_equal, op1=ALU.mult)
                        link.after(ins)
                        link.after(dve.tensor_reduce(which[:, :, n], rank[:], AX_X, ALU.max))
                        for t in range(NT):
                            ins = dve.tensor_scalar(ind[:, t, n, :], rank[:, t, :], which[:, t, n:n + 1], None, ALU.is_equal)
                        link.after(ins)
                        if n == 0:
                            for t in range(NT):
                                ins = dve.scalar_tensor_tensor(out=lg[:, t, :], in0=ind[:, t, 0, :], scalar=NEVER,
                                                               in1=lg[:, t, :], op0=ALU.mult, op1=ALU.add)
                            link.after(ins)
                    dve.tensor_tensor(diffs[:], top[:, :, 1], top[:, :, 0], ALU.subtract).then_inc(sem["diff_ready"], 1)
                    dve.wait_ge(sem["exp_ready"], b + 1)
                    link.after(dve.tensor_scalar(den[:], share[:, :, 1], 1.0, None, ALU.add))
                    link.after(dve.reciprocal(share[:, :, 0], den[:]))
                    dve.tensor_tensor(share[:, :, 1], share[:, :, 1], share[:, :, 0], ALU.mult).then_inc(sem["linked"], 1)
                    link.done += 1
                    for t in range(NT):
                        ins = dve.tensor_scalar(cw[:, t, :], ind[:, t, 0, :], share[:, t, 0:1], None, ALU.mult)
                    ins.then_inc(sem["linked"], 1)
                    link.done += 1
                    dve.wait_ge(sem["linked"], link.base + link.done)
                    for t in range(NT):
                        ins = dve.scalar_tensor_tensor(out=cw[:, t, :], in0=ind[:, t, 1, :], scalar=share[:, t, 1:2],
                                                       in1=cw[:, t, :], op0=ALU.mult, op1=ALU.add)
                    link.after(ins)
                    dve.wait_ge(fr.x_loaded[p], 16 * i + 16)
                    link.after(dve.tensor_copy(fr.total[:], fr.x[p][:]))
                    dve.sem_inc(sem["loop_dve"], 1)
                    with dve.Fori(0, E) as e:
                        n = (b * E + e) * 2
                        for t in range(NT):
                            dve.wait_ge(sem["silu_ready"], n + t + 1)
                            dve.tensor_tensor(hid[:, t, :], gu_ps[:, t, 1, 0:HID], silu[:, t, :], ALU.mult).then_inc(sem["hid_ready"], 1)
                        for t in range(NT):
                            dve.wait_ge(sem["y_ready"], n + t + 1)
                            dve.wait_ge(sem["y_used"], n + t + 2)
                            dve.scalar_tensor_tensor(out=fr.total[:, t, :], in0=y_ps[:, t, :], scalar=cw[:, t, bass.ds(e, 1)],
                                                     in1=fr.total[:, t, :], op0=ALU.mult, op1=ALU.add).then_inc(sem["y_used"], 1)
                    dve.wait_ge(sem["y_used"], 2 * E * (b + 1) + 2)
                    dve.nop().then_inc(fr.summed, 1)
                    fr.layer_norm(dve, link, i, p)

                batches(dve, batch)


def make_toeplitz(nc, filt, filt_pad, toeplitz):
    H = filt.shape[0]
    with ExitStack() as ctx:
        st = Stage(nc, ctx, "toep")
        kp = st.sb("kp", [H, P + D])
        padded, k_loaded, pad_stored = st.sem("padded"), st.sem("k_loaded"), st.sem("pad_stored")
        toep_stored = nc.alloc_semaphore("toep_stored")
        with nc.Block() as block:
            @block.gpsimd
            def _(pool):
                pool.memset(kp[:], 0.0).then_inc(padded, 1)

            @block.sync
            def _(sp):
                sp.wait_ge(padded, 1)
                sp.dma_start(kp[:, P:P + D], filt).then_inc(k_loaded, 16)
                sp.wait_ge(k_loaded, 16)
                sp.dma_start(filt_pad, kp[:]).then_inc(pad_stored, 16)
                sp.wait_ge(pad_stored, 16)
                rows_up = bass.AP(tensor=filt_pad.tensor, offset=filt_pad.offset + P,
                                  ap=[[P + D, H], [-1, P], [1, D]])
                sp.dma_start(toeplitz, rows_up).then_inc(toep_stored, 16)
    return toep_stored


def decoder_kernel(nc, a, out):
    x = [a["x"]] + [nc.dram_tensor(f"x_after_{k}", (B * S, D), F32, kind="Internal").ap() for k in range(5)] + [out]
    toeplitz = nc.dram_tensor("toeplitz", (32, P, D), F32, kind="Internal").ap()
    filt_pad = nc.dram_tensor("filt_pad", (32, P + D), F32, kind="Internal").ap()
    with ExitStack() as ctx:
        consts = make_constants(nc, ctx)
        toep_stored = make_toeplitz(nc, a["L0_xattn_k"], filt_pad, toeplitz)
        causal_heads_stage(nc, consts, "diff", x[0], x[1], {
            "wq": a["L0_attn_Wq"], "wk": a["L0_attn_Wk"], "wv": a["L0_attn_Wv"], "wo": a["L0_attn_Wo"],
            "lq1": a["L0_attn_lambda_q1"], "lk1": a["L0_attn_lambda_k1"], "lq2": a["L0_attn_lambda_q2"],
            "lk2": a["L0_attn_lambda_k2"], "lnw": a["L0_attn_ln_w"]}, "diff")
        long_conv_stage(nc, consts, "conv", x[1], x[2], a["ctx_2048"], toeplitz, toep_stored, a["fside_S2_0"])
        experts_stage(nc, consts, "moe", x[2], x[3], a["L0_ffn_router_w"], a["L0_ffn_gate_up_proj"], a["L0_ffn_down_proj"])
        causal_heads_stage(nc, consts, "plain", x[3], x[4], {
            "wq": a["wq"], "wk": a["wk"], "wv": a["wv"], "wo": a["L1_attn_w_o"]}, "plain")
        long_cross_stage(nc, consts, "cross", x[4], x[5], a["ctx_2048"], {
            "wq": a["L1_xattn_wq"], "wk": a["L1_xattn_wk"], "wv": a["L1_xattn_wv"], "wo": a["L1_xattn_wo"]})
        causal_heads_stage(nc, consts, "shared", x[5], x[6], {
            "wq": a["gq"], "wk": a["gk"], "wv": a["gv"], "wgate": a["L1_ffn_W_gate"]}, "shared")


_ROWS = ("x", "ctx_2048")
_PLAIN = ("fside_S2_0", "L0_attn_lambda_q1", "L0_attn_lambda_k1", "L0_attn_lambda_q2", "L0_attn_lambda_k2",
          "L0_attn_ln_w", "L0_xattn_k")
_TURNED = ("L0_attn_Wq", "L0_attn_Wk", "L0_attn_Wv", "L0_attn_Wo", "L0_ffn_gate_up_proj", "L0_ffn_down_proj",
           "L0_ffn_router_w", "L1_attn_w_qkv", "L1_attn_w_o", "L1_xattn_wq", "L1_xattn_wk", "L1_xattn_wv",
           "L1_xattn_wo", "L1_ffn_W_gate", "L1_ffn_W_qkv")


def kernel(**inputs):
    import numpy as _np
    import concourse.bacc as _bacc
    from concourse.bass_utils import run_bass_kernel_spmd as _run

    nc = _bacc.Bacc("TRN2", target_bir_lowering=False, num_devices=1)
    arrays, args = {}, {}
    for name in _ROWS + _PLAIN + _TURNED:
        a = _np.asarray(inputs[name])
        if name in _ROWS:
            a = a.reshape(B * S, D)
        elif name in _TURNED:
            a = _np.swapaxes(a, -1, -2)
        a = _np.ascontiguousarray(a)
        arrays[f"in_{name}"] = a
        args[name] = nc.dram_tensor(f"in_{name}", a.shape, mybir.dt.from_np(a.dtype), kind="ExternalInput").ap()
    for src, names in (("L1_attn_w_qkv", ("wq", "wk", "wv")), ("L1_ffn_W_qkv", ("gq", "gk", "gv"))):
        for n, name in enumerate(names):
            args[name] = args[src][:, n * D:(n + 1) * D]
    out = nc.dram_tensor("out_x", (B * S, D), F32, kind="ExternalOutput").ap()
    decoder_kernel(nc, args, out)
    r = _run(nc, [arrays], core_ids=[0])
    return r.results[0]["out_x"].reshape(B, S, D)
```

```python
from contextlib import ExitStack

import math

import concourse.bass as bass
from concourse import mybir

ALU = mybir.AluOpType
ACT = mybir.ActivationFunctionType
AX_X = mybir.AxisListType.X
F32 = mybir.dt.float32
BF16 = mybir.dt.bfloat16

P = 128
B = 8
S = 256
D = 512
NT = S // P
NC = D // P
EPS = 1e-5
MASKED = -1e30
NEVER = -3e38


class Stage:

    def __init__(self, nc, ctx, name):
        self.nc, self.ctx, self.name = nc, ctx, name
        ctx.callback(self.retire)
        self.sems = []

    def sb(self, name, shape, dt=F32):
        return self.ctx.enter_context(self.nc.sbuf_tensor(f"{self.name}_{name}", shape, dt))

    def ps(self, name, shape, dt=F32):
        return self.ctx.enter_context(self.nc.psum_tensor(f"{self.name}_{name}", shape, dt))

    def sem(self, name):
        s = self.nc.alloc_semaphore(f"{self.name}_{name}")
        self.sems.append(s)
        return s

    def retire(self):
        for s in self.sems:
            self.nc.gpsimd.sem_clear(s)
        self.nc.all_engine_barrier()
        for s in self.sems:
            self.nc.release_semaphore(s)


class Link:

    def __init__(self, eng, sem, per):
        self.eng, self.sem, self.per, self.done, self.base = eng, sem, per, 0, 0

    def start(self, b):
        assert self.done in (0, self.per), (self.done, self.per)
        self.base, self.done = b * self.per, 0

    def after(self, ins):
        ins.then_inc(self.sem, 1)
        self.done += 1
        self.eng.wait_ge(self.sem, self.base + self.done)


def make_constants(nc, ctx):
    st = Stage(nc, ctx, "const")
    c = {
        "ident": st.sb("ident", [P, P]),
        "ident_bf": st.sb("ident_bf", [P, P], BF16),
        "mask_bf": st.sb("mask_bf", [P, 4 * P], BF16),
    }
    c["minus_half"] = st.sb("minus_half", [P, NT * 16])
    c["octets"] = st.sb("octets", [P, P])
    c["strips"] = st.sb("strips", [P, P])
    filled, shaped = st.sem("filled"), st.sem("shaped")
    with nc.Block() as block:
        @block.gpsimd
        def _(pool):
            pool.memset(c["ident"][:], 0.0).then_inc(filled, 1)
            pool.memset(c["ident_bf"][:], 0.0).then_inc(filled, 1)
            pool.memset(c["mask_bf"][:], 0.0).then_inc(filled, 1)
            pool.memset(c["octets"][:], 1.0).then_inc(filled, 1)
            pool.memset(c["minus_half"][:], -0.5).then_inc(filled, 1)
            pool.memset(c["strips"][:], 1.0).then_inc(filled, 1)
            pool.wait_ge(filled, 6)
            for name in ("ident", "ident_bf"):
                pool.affine_select(out=c[name][:], in_=c[name][:], compare_op=ALU.not_equal, fill=1.0, base=0,
                                   pattern=[[-1, P]], channel_multiplier=1).then_inc(shaped, 1)
            pool.affine_select(out=c["mask_bf"][:], in_=c["mask_bf"][:], compare_op=ALU.is_ge, fill=MASKED, base=0,
                               pattern=[[0, 4], [-1, P]], channel_multiplier=1).then_inc(shaped, 1)
            pool.wait_ge(shaped, 3)
            for n, (name, r) in enumerate((("octets", 8), ("strips", 32))):
                m = c[name][:].rearrange("p (a r) -> p a r", r=r)
                pool.affine_select(out=m, in_=m, compare_op=ALU.is_ge, fill=0.0, base=0,
                                   pattern=[[-r, P // r], [0, r]], channel_multiplier=1).then_inc(shaped, 1)
                pool.wait_ge(shaped, 4 + 2 * n)
                pool.affine_select(out=m, in_=m, compare_op=ALU.is_ge, fill=0.0, base=r - 1,
                                   pattern=[[r, P // r], [0, r]], channel_multiplier=-1).then_inc(shaped, 1)
                pool.wait_ge(shaped, 5 + 2 * n)
    return c



def batches(eng, body):
    with eng.Fori(0, B // 2) as i:
        for p in range(2):
            body(i, p)


class Frame:

    def __init__(self, st, x_in, x_out, extra=None):
        self.st = st
        self.x_in = x_in.rearrange("(b t p) d -> b p t d", p=P, t=NT)
        self.x_out = x_out.rearrange("(b t p) d -> b p t d", p=P, t=NT)
        self.extra = None if extra is None else extra.rearrange("(b t p) d -> b p t d", p=P, t=NT)
        self.x = [st.sb(f"x{p}", [P, NT, D]) for p in range(2)]
        self.normed = [st.sb(f"normed{p}", [P, NT, D]) for p in range(2)]
        self.total = st.sb("total", [P, NT, D])
        self.stats = st.sb("stats", [P, NT, 6])
        self.moments = st.sb("moments", [P, NT, 2])
        self.rstd = st.sb("rstd", [P, NT])
        self.pause = st.sb("pause", [P, 1])
        self.x_loaded = [st.sem(f"x_loaded{p}") for p in range(2)]
        self.stored = [st.sem(f"stored{p}") for p in range(2)]
        self.summed = st.sem("summed")
        self.norm_done = st.sem("norm_done")
        self.var_ready = st.sem("var_ready")
        self.rstd_ready = st.sem("rstd_ready")
        self.carried = st.sem("carried_norm")
        if extra is not None:
            self.e = [st.sb(f"e{p}", [P, NT, D]) for p in range(2)]
            self.e_loaded = [st.sem(f"e_loaded{p}") for p in range(2)]

    def load(self, sp, b, p):
        sp.dma_start(self.x[p][:], self.x_in[b]).then_inc(self.x_loaded[p], 16)
        if self.extra is not None:
            sp.dma_start(self.e[p][:], self.extra[b]).then_inc(self.e_loaded[p], 16)

    def store(self, sp, b, p):
        sp.wait_ge(self.norm_done, b + 2)
        sp.dma_start(self.x_out[b], self.normed[p][:]).then_inc(self.stored[p], 16)

    def traffic(self, sp):
        for p in range(2):
            sp.sem_inc(self.stored[p], 16)
        sp.sem_inc(self.summed, 1)
        sp.sem_inc(self.norm_done, 1)
        for p in range(2):
            self.load(sp, p, p)
        with sp.Fori(0, B // 2 - 1) as i:
            for p in range(2):
                b = 2 * i + p
                sp.wait_ge(self.summed, b + 2)
                self.load(sp, b + 2, p)
                self.store(sp, b, p)
        for p in range(2):
            self.store(sp, B - 2 + p, p)
        for p in range(2):
            sp.wait_ge(self.stored[p], 16 * (B // 2 + 1))

    def root(self, pool, power, b):
        pool.wait_ge(self.var_ready, b + 1)
        pool.tensor_tensor(self.rstd[:], self.rstd[:], power[:, 0:NT], ALU.pow).then_inc(self.rstd_ready, 1)

    LINKS = 2

    def statistics(self, dve, link):
        for t in range(NT):
            ins = dve.bn_stats(self.stats[:, t, :], self.total[:, t, :])
        link.after(ins)
        dve.memset(self.pause[:], 0.0)
        for t in range(NT):
            ins = dve.bn_aggr(self.moments[:, t, :], self.stats[:, t, :])
        link.after(ins)
        dve.tensor_scalar(self.rstd[:], self.moments[:, :, 1], EPS, None, ALU.add).then_inc(self.var_ready, 1)

    def finish(self, eng, i, p):
        eng.wait_ge(self.rstd_ready, 2 * i + p + 1)
        eng.wait_ge(self.stored[p], 16 * i + 16)
        if eng is self.st.nc.gpsimd:
            eng.sem_inc(self.carried, 1)
        for t in range(NT):
            ins = eng.tensor_scalar(self.normed[p][:, t, :], self.total[:, t, :], self.moments[:, t, 0:1],
                                    self.rstd[:, t:t + 1], ALU.subtract, ALU.mult)
        ins.then_inc(self.norm_done, 1)

    def total_free(self, dve, b):
        dve.wait_ge(self.norm_done, b + 1)

    def norm_on_pool(self, pool, power, i, p):
        self.root(pool, power, 2 * i + p)
        self.finish(pool, i, p)


def transpose_rows(pe, ident, out, rows):
    for c in range(NC):
        for t in range(NT):
            ins = pe.transpose(out[:, c // 2, (c % 2) * S + t * P:(c % 2) * S + (t + 1) * P],
                               rows[:, t, c * P:(c + 1) * P], ident[:])
    return ins


def project_cols(pe, out, w, xT, col, n=P):
    for c in range(NC):
        ins = pe.matmul(out, w[:, c, col:col + n], xT[:, c, :], start=c == 0, stop=c == NC - 1)
    return ins


def project_rows(pe, out, xT, t, w, lo, hi):
    for c in range(NC):
        ins = pe.matmul(out, xT[:, c, t * P:(t + 1) * P], w[:, c, lo:hi], start=c == 0, stop=c == NC - 1)
    return ins


class Heads:

    BLOCKS = ((0, 0), (1, 1), (1, 0))

    def __init__(self, st, consts, units, scale, q_of, k_of, v_of, out_at, scores, probT_ps, outT_ps, merged):
        self.U, self.scale, self.merged = units, scale, merged
        self.q_of, self.k_of, self.v_of, self.out_at = q_of, k_of, v_of, out_at
        self.c = consts
        self.scores = scores.rearrange("p (u s) (k n) -> p u s k n", u=2, n=P)
        self.probT_ps, self.outT_ps = probT_ps, outT_ps
        self.slots = 1 if merged else 2
        self.probs = st.sb("probs", [P, 2, 2, 3, P])
        self.probT = st.sb("probT", [P, 2, 3, P])
        self.top = st.sb("top", [P, 2, 2, 2])
        self.shift = st.sb("shift", [P, 2, 2, 2])
        self.sums = st.sb("sums", [P, 4, 2, 2])
        self.inv = st.sb("inv", [P, 4, 2, 2])
        self.diag = st.sb("diag", [P, 2, 2, 2, P])
        self.scores_ready = st.sem("scores_ready")
        self.shift_ready = st.sem("shift_ready")
        self.probs_ready = st.sem("probs_ready")
        self.diag_ready = st.sem("diag_ready")
        self.probT_ready = st.sem("probT_ready")
        self.copied_act = st.sem("copied_act")
        self.copied_dve = st.sem("copied_dve")
        self.out_ready = st.sem("out_ready")

    def copied(self, eng, b, u, h):
        per = self.U * self.slots // 2
        k = u * self.slots + h
        eng.wait_ge(self.copied_dve if k % 2 else self.copied_act, b * per + k // 2 + 1)

    def score(self, pe, b, u):
        if u >= 2:
            pe.wait_ge(self.probs_ready, b * self.U + u - 1)
        masked = self.scores[:, u % 2, 0]
        pe.matmul(masked.rearrange("p k n -> p (k n)"), self.c["ident_bf"][:], self.c["mask_bf"][:],
                  start=True, stop=False)
        for h in range(2):
            for k, (t, kt) in enumerate(self.BLOCKS[0:2]):
                pe.matmul(masked[:, 2 * h + k], self.q_of(u, h, t), self.k_of(u, h, kt), start=False,
                          stop=h == 1 and k == 1)
        for h in range(2):
            ins = pe.matmul(self.scores[:, u % 2, 1, 2 * h + 1], self.q_of(u, h, 1), self.k_of(u, h, 0),
                            start=True, stop=True)
        ins.then_inc(self.scores_ready, 1)

    def turn(self, pe, b, u):
        pe.wait_ge(self.diag_ready, b * self.U + u + 1)
        if self.merged:
            if u >= 2:
                self.copied(pe, b, u - 2, 0)
            for k, (t, _) in enumerate(self.BLOCKS):
                for h in range(2):
                    ins = pe.matmul(self.probT_ps[:, u % 2, k * P:(k + 1) * P], self.probs[:, u % 2, h, k],
                                    self.diag[:, u % 2, t, h], start=h == 0, stop=h == 1)
            ins.then_inc(self.probT_ready, 1)
        else:
            for h in range(2):
                if u >= 1:
                    self.copied(pe, b, u - 1, h)
                for k, (t, _) in enumerate(self.BLOCKS):
                    ins = pe.matmul(self.probT_ps[:, h, k * P:(k + 1) * P], self.probs[:, u % 2, h, k],
                                    self.diag[:, u % 2, t, h], start=True, stop=True)
                ins.then_inc(self.probT_ready, 1)

    def weigh(self, pe, b, u):
        for h in range(self.slots):
            self.copied(pe, b, u, h)
            pT = self.probT[:, (u * self.slots + h) % 2]
            g, c = self.out_at(u, h)
            out = self.outT_ps[32 * g:32 * g + 32, c // 2, (c % 2) * S:(c % 2) * S + S]
            pe.matmul(out[:, 0:P], self.v_of(u, h, 0), pT[:, 0], start=True, stop=True)
            pe.matmul(out[:, P:S], self.v_of(u, h, 0), pT[:, 2], start=True, stop=False)
            ins = pe.matmul(out[:, P:S], self.v_of(u, h, 1), pT[:, 1], start=False, stop=True)
        ins.then_inc(self.out_ready, 1)

    def tensor(self, pe, b, summed):
        self.score(pe, b, 0)
        self.score(pe, b, 1)
        for u in range(self.U):
            if u + 2 < self.U:
                self.score(pe, b, u + 2)
            if u == 1:
                pe.wait_ge(summed, b + 1)
            if u >= 1:
                self.weigh(pe, b, u - 1)
            self.turn(pe, b, u)
        self.weigh(pe, b, self.U - 1)

    def exps(self, act, b, u):
        act.wait_ge(self.shift_ready, b * self.U + u + 1)
        if u >= 2:
            act.wait_ge(self.probT_ready, (b * self.U + u - 1) * self.slots)
        for h in range(2):
            act.activation(self.probs[:, u % 2, h, 0], self.scores[:, u % 2, 0, 2 * h], ACT.Exp,
                           bias=self.shift[:, u % 2, 0, h:h + 1], scale=self.scale,
                           accum_out=self.sums[:, u % 4, 0, h:h + 1])
            ins = act.activation(self.probs[:, u % 2, h, 1:3], self.scores[:, u % 2, :, 2 * h + 1], ACT.Exp,
                                 bias=self.shift[:, u % 2, 1, h:h + 1], scale=self.scale,
                                 accum_out=self.sums[:, u % 4, 1, h:h + 1])
        ins.then_inc(self.probs_ready, 1)

    def scalar(self, act, b):
        self.exps(act, b, 0)
        for u in range(self.U):
            if u + 1 < self.U:
                self.exps(act, b, u + 1)
            k = u * self.slots
            if k % 2 == 0:
                act.wait_ge(self.probT_ready, (b * self.U + u) * self.slots + 1)
                act.copy(self.probT[:, 0], self.probT_ps[:, 0, 0:3 * P].rearrange("p (k n) -> p k n", n=P)).then_inc(self.copied_act, 1)

    def maxima(self, dve, link, b, u):
        dve.wait_ge(self.scores_ready, b * self.U + u + 1)
        sc = self.scores[:, u % 2]
        dve.tensor_reduce(self.top[:, u % 2, 0, :], sc[:, 0, 0:4:2, :], AX_X, ALU.max)
        link.after(dve.tensor_reduce(self.top[:, u % 2, 1, :], sc[:, :, 1:4:2, :].rearrange("p s h n -> p h s n"),
                                     mybir.AxisListType.XY, ALU.max))
        dve.tensor_scalar(self.shift[:, u % 2], self.top[:, u % 2], -self.scale, None,
                          ALU.mult).then_inc(self.shift_ready, 1)

    LINKS_UNIT = 2

    def norms(self, dve, link, b, u, minus_lambda):
        dve.wait_ge(self.probs_ready, b * self.U + u + 1)
        inv = self.inv[:, u % 4]
        link.after(dve.reciprocal(inv, self.sums[:, u % 4]))
        if self.merged:
            link.after(dve.tensor_scalar(inv[:, :, 1], inv[:, :, 1], minus_lambda, None, ALU.mult))
        if u >= 2:
            dve.wait_ge(self.probT_ready, (b * self.U + u - 1) * self.slots)
        for t in range(2):
            for h in range(2):
                ins = dve.tensor_scalar(self.diag[:, u % 2, t, h], self.c["ident"][:], inv[:, t, h:h + 1], None, ALU.mult)
        ins.then_inc(self.diag_ready, 1)

    def vector(self, dve, link, b, minus_lambda=None):
        def copy(u):
            k = u * self.slots + self.slots - 1
            if k % 2:
                dve.wait_ge(self.probT_ready, b * self.U * self.slots + k + 1)
                dve.tensor_copy(self.probT[:, 1], self.probT_ps[:, 1, 0:3 * P].rearrange("p (k n) -> p k n", n=P)).then_inc(self.copied_dve, 1)

        self.maxima(dve, link, b, 0)
        self.maxima(dve, link, b, 1)
        for u in range(self.U):
            self.norms(dve, link, b, u, minus_lambda)
            if u + 2 < self.U:
                self.maxima(dve, link, b, u + 2)
            copy(u)


def causal_heads_stage(nc, consts, name, x_in, x_out, w, mode, norm_w=None):
    diff, plain, shared = mode == "diff", mode == "plain", mode == "shared"
    with ExitStack() as ctx:
        st = Stage(nc, ctx, name)
        fr = Frame(st, x_in, x_out)
        scores = st.ps("scores", [P, 4, 512])
        probT_ps = st.ps("probT_ps", [P, 2, 512])
        outT_ps = st.ps("outT_ps", [P, 2, 512])
        gate_ps = probT_ps[:, 0, :]
        xT = st.sb("xT", [P, NC, S])
        qT = st.sb("qT", [P, 4, S])
        mixedT = st.sb("mixedT", [P, NC, S])
        weights_loaded = st.sem("weights_loaded")
        weights_shaped = st.sem("weights_shaped")
        turned_ready = st.sem("turned_ready")
        turned_taken = st.sem("turned_taken")
        proj_ready = st.sem("proj_ready")
        proj_act = st.sem("proj_act")
        proj_dve = st.sem("proj_dve")
        mixed_ready = st.sem("mixed_ready")
        mixed_act = st.sem("mixed_act")
        mixed_normed = st.sem("mixed_normed")
        out_proj_ready = st.sem("out_proj_ready")
        linked = st.sem("linked")
        gate_linked = st.sem("gate_linked")
        k_turned = st.sem("k_turned")
        k_taken = st.sem("k_taken")
        k_picked = st.sem("k_picked")
        gate_used = st.sem("gate_used")
        gate_exp_in = st.sem("gate_exp_in")
        gate_exp_out = st.sem("gate_exp_out")

        loads = []
        n_loads = len(w)
        wide = {}
        for key, dram in w.items():
            if len(dram.shape) == 2:
                wide[key] = st.sb(key, [P, NC, dram.shape[1]])
                loads.append((wide[key][:], dram.rearrange("(c p) e -> p c e", p=P)))
            else:
                wide[key] = st.sb(key, [P, dram.shape[0]])
                loads.append((wide[key][:], dram.partition_broadcast(P)))

        if diff:
            lnw = st.sb("lnw", [P, 1])
            eps_ready = st.sem("eps_ready")
            for g in range(4):
                loads.append((lnw[32 * g:32 * g + 32, :], norm_w.rearrange("(p a) -> p a", a=1)))
            n_loads += 4
            H2, HD = 32, 16
            kT = st.sb("kT", [P, 8, S])
            v = st.sb("v", [P, NT, P])
            wkz = st.sb("wkz", [P, NC, 4, 2, P])
            lam = st.sb("lam", [P, 8])
            prod = st.sb("prod", [P, HD])
            square = st.sb("square", [P, NC, S])
            rms = st.sb("rms", [P, NC, S])
            eps = st.sb("eps", [P, 1])
            squared, square_summed, rms_ready = st.sem("squared"), st.sem("square_summed"), st.sem("rms_ready")
            lam_exp_in, lam_exp_out = st.sem("lam_exp_in"), st.sem("lam_exp_out")
            LAMBDA_INIT = 0.8 - 0.6 * math.exp(-0.3 * 12)
            jobs = [("qT", j) for j in range(2)] + [("kT", j) for j in range(4)] + [("v", 0)]
            units = 16
            scale = HD ** -0.5

            def q_of(u, h, t):
                g = u % 4
                return qT[32 * g:32 * g + 32, u // 4, t * P:(t + 1) * P]

            def k_of(u, h, kt):
                g = u % 4
                return kT[32 * g:32 * g + 32, 2 * (u // 4) + h, kt * P:(kt + 1) * P]

            def v_of(u, h, kt):
                return v[:, kt, 32 * (u // 4):32 * (u // 4) + 32]

            def out_at(u, h):
                return u % 4, u // 4
        else:
            HD = 32
            units = 8
            scale = HD ** -0.5

            def out_at(u, h):
                return u % 4, 2 * (u // 4) + h

            def q_of(u, h, t):
                g, c = out_at(u, h)
                return qT[32 * g:32 * g + 32, c, t * P:(t + 1) * P]
            if plain:
                kT = st.sb("kT", [P, 4, S])
                v = st.sb("v", [P, NT, D])
                jobs = [("qT", 0), ("qT", 1), ("kT", 0), ("kT", 1), ("v", 0), ("v", 1)]

                def k_of(u, h, kt):
                    g, c = out_at(u, h)
                    return kT[32 * g:32 * g + 32, c, kt * P:(kt + 1) * P]

                def v_of(u, h, kt):
                    g, c = out_at(u, h)
                    return v[:, kt, P * c + 32 * g:P * c + 32 * g + 32]
            else:
                NG = 16
                kT = st.sb("kT", [P, S])
                v = st.sb("v", [P, NT, 32])
                k4 = st.sb("k4", [P, NT, 4, 32])
                picked = st.sb("picked", [P, 2, D])
                descending = st.sb("descending", [P, NG])
                gl = st.sb("gl", [P, NT, NG])
                gtop = st.sb("gtop", [P, NT])
                gneg = st.sb("gneg", [P, NT])
                ind = st.sb("ind", [P, NT, NG])
                first = st.sb("first", [P, NT])
                gexp = st.sb("gexp", [P, NT, NG])
                gsum = st.sb("gsum", [P, NT])
                gval = st.sb("gval", [P, NT])
                indv = st.sb("indv", [P, NT, NG])
                iota_done = st.sem("iota_done")
                jobs = [("qT", 0), ("qT", 1)]

                def k_of(u, h, kt):
                    g = u % 4
                    return kT[32 * g:32 * g + 32, kt * P:(kt + 1) * P]

                def v_of(u, h, kt):
                    return v[:, kt, :]

        NJ = len(jobs)
        NJ_ACT, NJ_DVE = (NJ + 1) // 2, NJ // 2
        heads = Heads(st, consts, units, scale, q_of, k_of, v_of, out_at, scores[:], probT_ps,
                      outT_ps, merged=diff)
        LINKS = Heads.LINKS_UNIT * units + Frame.LINKS + (units + 2 if diff else 0)
        GATE_LINKS = 6 * NT + 3
        EARLY = 5
        FIRST_BANK = 2 if diff else 0

        def job_parts(j):
            kind, n = jobs[j]
            bank = scores[:, (FIRST_BANK + j) % 4, :]
            if kind == "v":
                return (bank[:, 0:2 * P], v[:].rearrange("p t d -> p (t d)")) if diff else (bank, v[:, n, :])
            dst = {"qT": qT, "kT": kT}[kind]
            return bank, dst[:, 2 * n:2 * n + 2, :].rearrange("p c s -> p (c s)")

        def overlapped(eng, batch):
            with eng.Fori(0, B // 2 - 1) as i:
                for p in range(2):
                    batch(2 * i + p, i, p, False)
            for p in range(2):
                batch(B - 2 + p, B // 2 - 1, p, p == 1)

        with nc.Block() as block:
            @block.sync
            def _(sp):
                for dst, src in loads:
                    sp.dma_start(dst, src).then_inc(weights_loaded, 16)
                fr.traffic(sp)

            @block.gpsimd
            def _(pool):
                if shared:
                    pool.iota(descending[:], [[-1, NG]], base=NG, channel_multiplier=0,
                              allow_small_or_imprecise_dtypes=True).then_inc(iota_done, 1)

                def batch(i, p):
                    fr.norm_on_pool(pool, consts["minus_half"], i, p)
                batches(pool, batch)

            @block.tensor
            def _(pe):
                pe.wait_ge(weights_loaded, 16 * n_loads)
                if diff:
                    pe.wait_ge(weights_shaped, 1)

                def turn_x(b, i, p):
                    pe.wait_ge(fr.x_loaded[p], 16 * i + 16)
                    transpose_rows(pe, consts["ident"], probT_ps, fr.x[p]).then_inc(turned_ready, 1)

                def project(b, lo, hi, first):
                    for j in range(lo, hi):
                        kind, n = jobs[j]
                        if j >= 4:
                            if j % 2:
                                pe.wait_ge(proj_dve, NJ_DVE * b + (j - 4) // 2 + 1)
                            else:
                                pe.wait_ge(proj_act, NJ_ACT * b + (j - 4) // 2 + 1)
                        elif diff and j == 2 and not first:
                            pe.wait_ge(rms_ready, b)
                        bank = scores[:, (FIRST_BANK + j) % 4, :]
                        if kind == "v":
                            if diff:
                                for t in range(NT):
                                    ins = project_rows(pe, bank[:, t * P:(t + 1) * P], xT, t, wide["wv"], 0, P)
                            else:
                                ins = project_rows(pe, bank, xT, n, wide["wv"], 0, D)
                        else:
                            for h in range(2):
                                out = bank[:, h * S:(h + 1) * S]
                                if diff and kind == "kT":
                                    for c in range(NC):
                                        ins = pe.matmul(out, wkz[:, c, n, h, :], xT[:, c, :],
                                                        start=c == 0, stop=c == NC - 1)
                                else:
                                    ins = project_cols(pe, out, wide["w" + kind[0]], xT, (2 * n + h) * P)
                        ins.then_inc(proj_ready, 1)

                def project_shared(b, first):
                    for t in range(NT):
                        if t == 1:
                            pe.wait_ge(k_picked, 2 * b + 1)
                        project_rows(pe, gate_ps[:, 0:NG], xT, t, wide["wgate"], 0, NG)
                        project_rows(pe, scores[:, 2, :], xT, t, wide["wk"], 0, D)
                        project_rows(pe, scores[:, 3, :], xT, t, wide["wv"], 0, D).then_inc(gate_used, 1)
                        project(b, t, t + 1, first)
                    pe.wait_ge(k_picked, 2 * b + 2)
                    for t in range(NT):
                        ins = pe.transpose(gate_ps[:, P + t * P:P + (t + 1) * P],
                                           k4[:, t].rearrange("p g d -> p (g d)"), consts["ident"][:])
                    ins.then_inc(k_turned, 1)
                    pe.wait_ge(k_taken, b + 1)

                def project_all(b, first):
                    pe.wait_ge(turned_taken, b + 1)
                    if shared:
                        project_shared(b, first)
                    else:
                        project(b, 0, NJ, first)

                def result(b):
                    for t in range(NT):
                        if shared:
                            for c in range(NC):
                                ins = pe.transpose(outT_ps[:, t, c * P:(c + 1) * P], mixedT[:, c, t * P:(t + 1) * P],
                                                   consts["ident"][:])
                        else:
                            ins = project_rows(pe, outT_ps[:, t, :], mixedT, t, wide["wo"], 0, D)
                        ins.then_inc(out_proj_ready, 1)

                def batch(b, i, p, last):
                    pe.wait_ge(proj_act, NJ_ACT * (b + 1))
                    pe.wait_ge(proj_dve, NJ_DVE * (b + 1))
                    heads.tensor(pe, b, fr.summed)
                    if not last:
                        turn_x(b + 1, i + p, 1 - p)
                    pe.wait_ge(mixed_act, b + 1)
                    pe.wait_ge(mixed_ready, b + 1)
                    if diff:
                        for c in range(NC):
                            ins = pe.matmul(scores[:, c // 2, (c % 2) * S:(c % 2 + 1) * S], consts["strips"][:], square[:, c],
                                            start=True, stop=True)
                        ins.then_inc(square_summed, 1)
                        if not last:
                            pe.wait_ge(turned_taken, b + 2)
                            project(b + 1, 0, EARLY, False)
                        pe.wait_ge(mixed_normed, b + 1)
                        result(b)
                        if not last:
                            project(b + 1, EARLY, NJ, False)
                    else:
                        result(b)
                        if not last:
                            project_all(b + 1, False)

                turn_x(0, 0, 0)
                project_all(0, True)
                overlapped(pe, batch)

            @block.scalar
            def _(act):
                if diff:
                    act.wait_ge(eps_ready, 1)
                    act.wait_ge(lam_exp_in, 1)
                    act.activation(lam[:, 2:4], lam[:, 0:2], ACT.Exp).then_inc(lam_exp_out, 1)

                def take_turned(b):
                    act.wait_ge(turned_ready, b + 1)
                    act.copy(xT[:].rearrange("p (a c) s -> p a (c s)", a=2), probT_ps[:]).then_inc(turned_taken, 1)

                def take_projections(b):
                    if shared:
                        act.wait_ge(gate_exp_in, b + 1)
                        act.activation(gexp[:], gl[:], ACT.Exp).then_inc(gate_exp_out, 1)
                    for j in range(0, NJ, 2):
                        src, dst = job_parts(j)
                        act.wait_ge(proj_ready, NJ * b + j + 1)
                        act.copy(dst, src).then_inc(proj_act, 1)
                    if shared:
                        act.wait_ge(k_turned, b + 1)
                        act.copy(kT[:], gate_ps[:, P:P + S]).then_inc(k_taken, 1)

                def batch(b, i, p, last):
                    heads.scalar(act, b)
                    act.wait_ge(heads.out_ready, units * b + units // 2)
                    act.copy(mixedT[:, 0:2], outT_ps[:, 0, :].rearrange("p (c s) -> p c s", c=2)).then_inc(mixed_act, 1)
                    if not last:
                        take_turned(b + 1)
                    if diff:
                        act.wait_ge(square_summed, b + 1)
                        act.activation(rms[:], scores[:, 0:2, :].rearrange("p a (c s) -> p (a c) s", c=2), ACT.Sqrt,
                                       bias=eps[:], scale=1.0 / 32).then_inc(rms_ready, 1)
                    if not last:
                        take_projections(b + 1)

                take_turned(0)
                take_projections(0)
                overlapped(act, batch)

            @block.vector
            def _(dve):
                link = Link(dve, linked, LINKS)
                setup = 0
                if diff or shared:
                    dve.wait_ge(weights_loaded, 16 * n_loads)
                if diff:
                    shaped = st.sem("shaped")
                    setup_link = Link(dve, shaped, 1 << 30)
                    setup_link.after(dve.memset(wkz[:], 0.0))
                    wk = wide["wk"][:].rearrange("p n (c j k) -> p n c j k", c=4, j=2)
                    for s in range(2):
                        for g in range(4):
                            lo = 32 * g + 16 * s
                            ins = dve.tensor_copy(wkz[:, :, :, s, lo:lo + 16], wk[:, :, :, g // 2, :])
                    ins.then_inc(weights_shaped, 1)
                    for n in range(2):
                        setup_link.after(dve.tensor_tensor(prod[:], wide[f"lq{n + 1}"][:], wide[f"lk{n + 1}"][:], ALU.mult))
                        setup_link.after(dve.tensor_reduce(lam[:, n:n + 1], prod[:], AX_X, ALU.add))
                    setup_link.after(dve.tensor_scalar(lnw[:], lnw[:], 1.0 - LAMBDA_INIT, None, ALU.mult))
                    dve.memset(eps[:], EPS).then_inc(eps_ready, 1)
                    dve.nop().then_inc(lam_exp_in, 1)
                    dve.wait_ge(lam_exp_out, 1)
                    setup_link.after(dve.tensor_tensor(lam[:, 4:5], lam[:, 3:4], lam[:, 2:3], ALU.subtract))
                    setup_link.after(dve.tensor_scalar(lam[:, 5:6], lam[:, 4:5], -LAMBDA_INIT, None, ALU.add))
                if shared:
                    dve.wait_ge(iota_done, 1)

                gate_link = Link(dve, gate_linked, GATE_LINKS)

                def pick(b):
                    gate_link.start(b)
                    for t in range(NT):
                        dve.wait_ge(gate_used, 2 * b + t + 1)
                        gate = gate_ps[:, 0:NG]
                        gate_link.after(dve.tensor_reduce(gtop[:, t:t + 1], gate, AX_X, ALU.max))
                        dve.tensor_scalar(gl[:, t, :], gate, gtop[:, t:t + 1], None, ALU.subtract)
                        gate_link.after(dve.scalar_tensor_tensor(out=ind[:, t, :], in0=gate, scalar=gtop[:, t:t + 1],
                                                            in1=descending[:], op0=ALU.is_equal, op1=ALU.mult))
                        gate_link.after(dve.tensor_reduce(first[:, t:t + 1], ind[:, t, :], AX_X, ALU.max))
                        gate_link.after(dve.tensor_scalar(ind[:, t, :], ind[:, t, :], first[:, t:t + 1], None, ALU.is_equal))
                        for n, bank in enumerate((2, 3)):
                            ins = dve.tensor_tensor(
                                picked[:, n, :].rearrange("p (h d) -> p h d", d=HD),
                                scores[:, bank, :].rearrange("p (h d) -> p h d", d=HD),
                                ind[:, t, :].unsqueeze(2).to_broadcast([P, NG, HD]), ALU.mult)
                        gate_link.after(ins)
                        dve.tensor_reduce(v[:, t, :], picked[:, 1, :].rearrange("p (h d) -> p d h", d=HD), AX_X, ALU.add)
                        gate_link.after(dve.tensor_reduce(k4[:, t, 0, :], picked[:, 0, :].rearrange("p (h d) -> p d h", d=HD),
                                                     AX_X, ALU.add))
                        dve.tensor_copy(k4[:, t, 1:4, :], k4[:, t, 0:1, :].to_broadcast([P, 3, HD])).then_inc(k_picked, 1)
                    dve.nop().then_inc(gate_exp_in, 1)
                    dve.wait_ge(gate_exp_out, b + 1)
                    gate_link.after(dve.tensor_reduce(gsum[:], gexp[:], AX_X, ALU.add))
                    gate_link.after(dve.reciprocal(gval[:], gsum[:]))
                    for t in range(NT):
                        ins = dve.tensor_scalar(v[:, t, :], v[:, t, :], gval[:, t:t + 1], None, ALU.mult)
                    gate_link.after(ins)

                def take_projections(b, lo=0, hi=NJ):
                    if shared:
                        pick(b)
                    for j in range(lo, hi):
                        if j % 2:
                            src, dst = job_parts(j)
                            dve.wait_ge(proj_ready, NJ * b + j + 1)
                            dve.tensor_copy(dst, src).then_inc(proj_dve, 1)

                def batch(b, i, p, last):
                    link.start(b)
                    heads.vector(dve, link, b, lam[:, 5:6] if diff else None)
                    dve.wait_ge(heads.out_ready, units * (b + 1))
                    ins = dve.tensor_copy(mixedT[:, 2:4], outT_ps[:, 1, :].rearrange("p (c s) -> p c s", c=2))
                    if diff:
                        link.after(ins)
                        dve.wait_ge(mixed_act, b + 1)
                        dve.tensor_tensor(square[:], mixedT[:], mixedT[:], ALU.mult).then_inc(mixed_ready, 1)
                        dve.wait_ge(rms_ready, b + 1)
                        link.after(dve.reciprocal(rms[:], rms[:]))
                        dve.scalar_tensor_tensor(out=mixedT[:], in0=mixedT[:], scalar=lnw[:, 0:1], in1=rms[:],
                                                 op0=ALU.mult, op1=ALU.mult).then_inc(mixed_normed, 1)
                        if not last:
                            take_projections(b + 1, 0, EARLY)
                    else:
                        ins.then_inc(mixed_ready, 1)
                    fr.total_free(dve, b)
                    for t in range(NT):
                        dve.wait_ge(out_proj_ready, 2 * b + t + 1)
                        ins = dve.tensor_tensor(fr.total[:, t, :], outT_ps[:, t, :], fr.x[p][:, t, :], ALU.add)
                    ins.then_inc(fr.summed, 1)
                    dve.wait_ge(fr.summed, b + 2)
                    fr.statistics(dve, link)
                    if not last:
                        take_projections(b + 1, EARLY if diff else 0)

                take_projections(0)
                overlapped(dve, batch)



def long_conv_stage(nc, consts, name, x_in, x_out, ctx_in, toeplitz, toep_stored, skip):
    H, NI = 32, 8
    with ExitStack() as ctx:
        st = Stage(nc, ctx, name)
        vT = st.sb("vT", [P, NC, B, S])
        cT = st.sb("cT", [P, NC, B, S])

        with ExitStack() as ctx_a:
            sa = Stage(nc, ctx_a, name + "A")
            src = [[sa.sb(f"src{p}{n}", [P, NT, D]) for n in range(2)] for p in range(2)]
            ps = [sa.ps(f"ps{n}", [P, 2, 512]) for n in range(2)]
            loaded = [[sa.sem(f"loaded{p}{n}") for n in range(2)] for p in range(2)]
            turned = [sa.sem(f"turned{n}") for n in range(2)]
            taken = [sa.sem(f"taken{n}") for n in range(2)]
            rows = [a.rearrange("(b t p) d -> b p t d", p=P, t=NT) for a in (x_in, ctx_in)]
            with nc.Block() as block:
                @block.sync
                def _(sp):
                    for p in range(2):
                        for n in range(2):
                            sp.dma_start(src[p][n][:], rows[n][p]).then_inc(loaded[p][n], 16)
                    with sp.Fori(0, B // 2 - 1) as i:
                        for p in range(2):
                            for n in range(2):
                                sp.wait_ge(turned[n], 2 * i + p + 1)
                                sp.dma_start(src[p][n][:], rows[n][2 * i + p + 2]).then_inc(loaded[p][n], 16)

                @block.tensor
                def _(pe):
                    for n in range(2):
                        pe.sem_inc(taken[n], 1)

                    def batch(i, p):
                        for n in range(2):
                            pe.wait_ge(loaded[p][n], 16 * i + 16)
                            pe.wait_ge(taken[n], 2 * i + p + 1)
                            transpose_rows(pe, consts["ident"], ps[n], src[p][n]).then_inc(turned[n], 1)
                    batches(pe, batch)

                @block.scalar
                def _(act):
                    def batch(i, p):
                        act.wait_ge(turned[0], 2 * i + p + 1)
                        act.copy(vT[:, :, 2 * i + p, :],
                                 ps[0][:].rearrange("p a (c s) -> p (a c) s", c=2)).then_inc(taken[0], 1)
                    batches(act, batch)

                @block.vector
                def _(dve):
                    def batch(i, p):
                        dve.wait_ge(turned[1], 2 * i + p + 1)
                        dve.tensor_copy(cT[:, :, 2 * i + p, :],
                                        ps[1][:].rearrange("p a (c s) -> p (a c) s", c=2)).then_inc(taken[1], 1)
                    batches(dve, batch)

        with ExitStack() as ctx_b:
            sb_ = Stage(nc, ctx_b, name + "B")
            toep = [sb_.sb(f"toep{p}", [P, D]) for p in range(2)]
            kv = [sb_.sb(f"kv{p}", [P, NC, B, NI, NI]) for p in range(2)]
            prod = sb_.sb("prod", [P, 2, B, NI, NI])
            conv = sb_.ps("conv", [P, 8, 512])
            toep_loaded = [sb_.sem(f"toep_loaded{p}") for p in range(2)]
            kv_ready = sb_.sem("kv_ready")
            conv_ready = sb_.sem("conv_ready")
            prod_ready = sb_.sem("prod_ready")

            def pairs_of(buf, c, h, over):
                a = buf[:, c, :, bass.ds(h * NI, NI)]
                return a.unsqueeze(3 if over == "i" else 2).to_broadcast([P, B, NI, NI])

            def heads_loop(eng, body):
                for p in range(2):
                    body(p, p, False)
                with eng.Fori(1, H // 2) as i:
                    for p in range(2):
                        body(2 * i + p, p, True)

            with nc.Block() as block:
                @block.sync
                def _(sp):
                    sp.wait_ge(toep_stored, 16)

                    def head(h, p, steady):
                        if steady:
                            sp.wait_ge(conv_ready, NC * h - NC)
                        sp.dma_start(toep[p][:], toeplitz[h]).then_inc(toep_loaded[p], 16)
                    heads_loop(sp, head)

                @block.gpsimd
                def _(pool):
                    def head(h, p, steady):
                        if steady:
                            pool.wait_ge(conv_ready, NC * h - NC)
                        for c in range(NC):
                            pool.tensor_tensor(kv[p][:, c], pairs_of(vT, c, h, "i"), pairs_of(cT, c, h, "j"),
                                               ALU.mult).then_inc(kv_ready, 1)
                    heads_loop(pool, head)

                @block.tensor
                def _(pe):
                    def head(h, p, steady):
                        pe.wait_ge(toep_loaded[p], h * 8 + 16 - 8 * p)
                        for lc in range(NC):
                            pe.wait_ge(kv_ready, NC * h + lc + 1)
                            if steady:
                                pe.wait_ge(prod_ready, NC * h + lc + 1 - 2 * NC)
                            for c in range(lc + 1):
                                lo = (lc - c) * P
                                ins = pe.matmul(conv[:, NC * p + lc, :], toep[p][:, lo:lo + P],
                                                kv[p][:, c].rearrange("p b i j -> p (b i j)"),
                                                start=c == 0, stop=c == lc)
                            ins.then_inc(conv_ready, 1)
                    heads_loop(pe, head)

                @block.vector
                def _(dve):
                    def head(h, p, steady):
                        for lc in range(NC):
                            dve.wait_ge(conv_ready, NC * h + lc + 1)
                            bank = conv[:, NC * p + lc, :].rearrange("p (b i j) -> p b i j", i=NI, j=NI)
                            dve.tensor_tensor(prod[:, lc % 2], bank, pairs_of(cT, lc, h, "i"),
                                              ALU.mult).then_inc(prod_ready, 1)
                            dve.wait_ge(prod_ready, NC * h + lc + 1)
                            dve.tensor_reduce(vT[:, lc, :, bass.ds(h * NI, NI)],
                                              prod[:, lc % 2].rearrange("p b i j -> p b j i"), AX_X, ALU.add)
                    heads_loop(dve, head)

        with ExitStack() as ctx_c:
            sc = Stage(nc, ctx_c, name + "C")
            fr = Frame(sc, x_in, x_out, ctx_in)
            skips = sc.sb("skips", [P, NT])
            skipped = sc.sb("skipped", [P, NT, D])
            part = sc.sb("part", [P, NT, D])
            result = sc.sb("result", [P, NC, S])
            back = [sc.ps(f"back{p}", [P, NT, 512]) for p in range(2)]
            osum = [sc.ps(f"osum{p}", [P, NT, 512]) for p in range(2)]
            skip_loaded = sc.sem("skip_loaded")
            result_copied, skipped_ready = sc.sem("result_copied"), sc.sem("skipped_ready")
            back_ready, osum_ready, linked = sc.sem("back_ready"), sc.sem("osum_ready"), sc.sem("linked")
            with nc.Block() as block:
                @block.sync
                def _(sp):
                    sp.dma_start(skips[:], skip.rearrange("(t p) -> p t", p=P), allow_slow_non_contiguous=True).then_inc(skip_loaded, 16)
                    fr.traffic(sp)

                @block.gpsimd
                def _(pool):
                    batches(pool, lambda i, p: fr.norm_on_pool(pool, consts["minus_half"], i, p))

                @block.scalar
                def _(act):
                    act.sem_inc(back_ready, 1)

                    def batch(i, p):
                        b = 2 * i + p
                        act.wait_ge(back_ready, b + 1)
                        act.copy(result[:], vT[:, :, b, :]).then_inc(result_copied, 1)
                    batches(act, batch)

                @block.tensor
                def _(pe):
                    def batch(i, p):
                        b = 2 * i + p
                        pe.wait_ge(result_copied, b + 1)
                        pe.wait_ge(fr.summed, b + 1)
                        for t in range(NT):
                            for c in range(NC):
                                ins = pe.transpose(back[p][:, t, c * P:(c + 1) * P], result[:, c, t * P:(t + 1) * P],
                                                   consts["ident"][:])
                        ins.then_inc(back_ready, 1)
                        pe.wait_ge(skipped_ready, b + 1)
                        for t in range(NT):
                            ins = pe.matmul(osum[p][:, t, :], consts["octets"][:], skipped[:, t, :], start=True, stop=True)
                        ins.then_inc(osum_ready, 1)
                    batches(pe, batch)

                @block.vector
                def _(dve):
                    link = Link(dve, linked, Frame.LINKS + 1)
                    dve.wait_ge(skip_loaded, 16)

                    def batch(i, p):
                        b = 2 * i + p
                        link.start(b)
                        dve.wait_ge(fr.x_loaded[p], 16 * i + 16)
                        dve.wait_ge(fr.e_loaded[p], 16 * i + 16)
                        for t in range(NT):
                            ins = dve.scalar_tensor_tensor(out=skipped[:, t, :], in0=fr.x[p][:, t, :], scalar=skips[:, t:t + 1],
                                                           in1=fr.e[p][:, t, :], op0=ALU.mult, op1=ALU.mult)
                        ins.then_inc(skipped_ready, 1)
                        dve.wait_ge(back_ready, b + 2)
                        dve.tensor_tensor(part[:], back[p][:], fr.x[p][:], ALU.add)
                        dve.wait_ge(osum_ready, b + 1)
                        fr.total_free(dve, b)
                        link.after(dve.tensor_tensor(fr.total[:], osum[p][:], fr.e[p][:], ALU.mult))
                        dve.tensor_tensor(fr.total[:], fr.total[:], part[:], ALU.add).then_inc(fr.summed, 1)
                        dve.wait_ge(fr.summed, b + 2)
                        fr.statistics(dve, link)
                    batches(dve, batch)


def long_cross_stage(nc, consts, name, x_in, x_out, ctx_in, w):
    KT = 2 * NT
    SCALE = 1.0 / math.sqrt(D)
    with ExitStack() as ctx:
        st = Stage(nc, ctx, name)
        fr = Frame(st, x_in, x_out, ctx_in)
        banks = st.ps("banks", [P, 4, 512])
        turn_ps = st.ps("turn_ps", [P, 2, 2, 512])
        xT = st.sb("xT", [P, NC, S])
        qT = st.sb("qT", [P, NC, S])
        kT = st.sb("kT", [P, NC, 2 * S])
        v = st.sb("v", [P, NT, D])
        probs = st.sb("probs", [P, NT, 2 * S])
        probT = st.sb("probT", [P, NT, KT, P])
        mixed = st.sb("mixed", [P, NT, D])
        top, shift, sums, inv = (st.sb(n, [P, NT]) for n in ("top", "shift", "sums", "inv"))
        wide = {k: st.sb(k, [P, NC, D]) for k in w}
        sem = {n: st.sem(n) for n in (
            "weights_loaded", "x_turned", "x_taken", "e_turned", "e_taken", "proj_ready", "proj_act", "proj_dve",
            "scores_ready", "shift_ready", "probs_ready", "probs_turned", "probT_act", "probT_dve", "mixed_raw",
            "mixed_ready", "mixed_turned", "mixed_taken", "out_ready", "linked")}
        LINKS = Frame.LINKS + 3
        with nc.Block() as block:
            @block.sync
            def _(sp):
                for k in w:
                    sp.dma_start(wide[k][:], w[k].rearrange("(c p) e -> p c e", p=P)).then_inc(sem["weights_loaded"], 16)
                fr.traffic(sp)

            @block.tensor
            def _(pe):
                pe.wait_ge(sem["weights_loaded"], 16 * len(w))

                def batch(i, p):
                    b = 2 * i + p
                    pe.wait_ge(fr.x_loaded[p], 16 * i + 16)
                    transpose_rows(pe, consts["ident"], turn_ps[:, 0], fr.x[p]).then_inc(sem["x_turned"], 1)
                    pe.wait_ge(fr.e_loaded[p], 16 * i + 16)
                    transpose_rows(pe, consts["ident"], turn_ps[:, 1], fr.e[p]).then_inc(sem["e_turned"], 1)
                    pe.wait_ge(sem["x_taken"], b + 1)
                    pe.wait_ge(fr.summed, b + 1)
                    for j in range(4):
                        for h in range(2):
                            ins = project_cols(pe, banks[:, j, h * S:(h + 1) * S], wide["wq" if j < 2 else "wk"], xT,
                                               (2 * (j % 2) + h) * P)
                        ins.then_inc(sem["proj_ready"], 1)
                    for t in range(NT):
                        pe.wait_ge(sem["proj_dve"] if t else sem["proj_act"], 3 * b + 1)
                        project_rows(pe, banks[:, t, :], xT, t, wide["wv"], 0, D).then_inc(sem["proj_ready"], 1)
                    pe.wait_ge(sem["e_taken"], b + 1)
                    pe.wait_ge(sem["proj_act"], 3 * b + 2)
                    pe.wait_ge(sem["proj_dve"], 3 * b + 2)
                    for t in range(NT):
                        for c in range(NC):
                            ins = pe.matmul(banks[:, 2 + t, :], qT[:, c, t * P:(t + 1) * P], kT[:, c, :],
                                            start=c == 0, stop=c == NC - 1)
                        ins.then_inc(sem["scores_ready"], 1)
                    for t in range(NT):
                        pe.wait_ge(sem["probs_ready"], 2 * b + t + 1)
                        for k in range(KT):
                            ins = pe.transpose(turn_ps[:, 0, t, k * P:(k + 1) * P], probs[:, t, k * P:(k + 1) * P],
                                               consts["ident"][:])
                        ins.then_inc(sem["probs_turned"], 1)
                    pe.wait_ge(sem["proj_act"], 3 * b + 3)
                    pe.wait_ge(sem["proj_dve"], 3 * b + 3)
                    for t in range(NT):
                        pe.wait_ge(sem["probT_dve"] if t else sem["probT_act"], b + 1)
                        for k in range(KT):
                            val = fr.e[p][:, k, :] if k < NT else v[:, k - NT, :]
                            ins = pe.matmul(banks[:, t, :], probT[:, t, k, :], val, start=k == 0, stop=k == KT - 1)
                        ins.then_inc(sem["mixed_raw"], 1)
                    pe.wait_ge(sem["mixed_ready"], b + 1)
                    transpose_rows(pe, consts["ident"], turn_ps[:, 1], mixed).then_inc(sem["mixed_turned"], 1)
                    pe.wait_ge(sem["mixed_taken"], b + 1)
                    for t in range(NT):
                        project_rows(pe, banks[:, 2 + t, :], xT, t, wide["wo"], 0, D).then_inc(sem["out_ready"], 1)

                batches(pe, batch)

            def turned(half, dst):
                return dst.rearrange("p (a c) s -> p a c s", a=2), turn_ps[:, half].rearrange("p a (c s) -> p a c s", c=2)

            @block.gpsimd
            def _(pool):
                batches(pool, lambda i, p: fr.norm_on_pool(pool, consts["minus_half"], i, p))

            @block.scalar
            def _(act):
                def batch(i, p):
                    b = 2 * i + p
                    act.wait_ge(sem["x_turned"], b + 1)
                    act.copy(*turned(0, xT[:])).then_inc(sem["x_taken"], 1)
                    for n, dst in enumerate((qT[:, 0:2, :], kT[:, 0:2, S:2 * S], None)):
                        act.wait_ge(sem["proj_ready"], 6 * b + 2 * n + 1)
                        if n < 2:
                            act.copy(dst, banks[:, 2 * n, :].rearrange("p (c s) -> p c s", c=2)).then_inc(sem["proj_act"], 1)
                        else:
                            act.copy(v[:, 0, :], banks[:, 0, :]).then_inc(sem["proj_act"], 1)
                    for t in range(NT):
                        act.wait_ge(sem["shift_ready"], 2 * b + t + 1)
                        act.activation(probs[:, t, :], banks[:, 2 + t, :], ACT.Exp, bias=shift[:, t:t + 1], scale=SCALE,
                                       accum_out=sums[:, t:t + 1]).then_inc(sem["probs_ready"], 1)
                    act.wait_ge(sem["probs_turned"], 2 * b + 1)
                    act.copy(probT[:, 0].rearrange("p k q -> p (k q)"), turn_ps[:, 0, 0, :]).then_inc(sem["probT_act"], 1)
                    act.wait_ge(sem["mixed_turned"], b + 1)
                    act.copy(*turned(1, xT[:])).then_inc(sem["mixed_taken"], 1)

                batches(act, batch)

            @block.vector
            def _(dve):
                link = Link(dve, sem["linked"], LINKS)

                def batch(i, p):
                    b = 2 * i + p
                    link.start(b)
                    dve.wait_ge(sem["e_turned"], b + 1)
                    dst, src = turned(1, kT[:, :, 0:S])
                    for a in range(2):
                        ins = dve.tensor_copy(dst[:, a], src[:, a])
                    ins.then_inc(sem["e_taken"], 1)
                    for n, dst in enumerate((qT[:, 2:4, :], kT[:, 2:4, S:2 * S], None)):
                        dve.wait_ge(sem["proj_ready"], 6 * b + 2 * n + 2)
                        if n < 2:
                            dve.tensor_copy(dst, banks[:, 2 * n + 1, :].rearrange("p (c s) -> p c s", c=2)).then_inc(sem["proj_dve"], 1)
                        else:
                            dve.tensor_copy(v[:, 1, :], banks[:, 1, :]).then_inc(sem["proj_dve"], 1)
                    for t in range(NT):
                        dve.wait_ge(sem["scores_ready"], 2 * b + t + 1)
                        link.after(dve.tensor_reduce(top[:, t:t + 1], banks[:, 2 + t, :], AX_X, ALU.max))
                        dve.tensor_scalar(shift[:, t:t + 1], top[:, t:t + 1], -SCALE, None, ALU.mult).then_inc(sem["shift_ready"], 1)
                    dve.wait_ge(sem["probs_turned"], 2 * b + 2)
                    dve.tensor_copy(probT[:, 1].rearrange("p k q -> p (k q)"), turn_ps[:, 0, 1, :]).then_inc(sem["probT_dve"], 1)
                    link.after(dve.reciprocal(inv[:], sums[:]))
                    for t in range(NT):
                        dve.wait_ge(sem["mixed_raw"], 2 * b + t + 1)
                        ins = dve.tensor_scalar(mixed[:, t, :], banks[:, t, :], inv[:, t:t + 1], None, ALU.mult)
                    ins.then_inc(sem["mixed_ready"], 1)
                    fr.total_free(dve, b)
                    for t in range(NT):
                        dve.wait_ge(sem["out_ready"], 2 * b + t + 1)
                        ins = dve.tensor_tensor(fr.total[:, t, :], banks[:, 2 + t, :], fr.x[p][:, t, :], ALU.add)
                    ins.then_inc(fr.summed, 1)
                    dve.wait_ge(fr.summed, b + 2)
                    fr.statistics(dve, link)

                batches(dve, batch)


def experts_stage(nc, consts, name, x_in, x_out, w_router, w_gu, w_down):
    E, HID = 8, 352
    HC = [(0, P), (P, P), (2 * P, HID - 2 * P)]
    T = B * NT
    PICKS = 2
    FULL = PICKS * T + E - 1
    TILES = FULL + FULL % 2
    U32 = mybir.dt.uint32
    token_of = nc.dram_tensor("token_of", (TILES * P, 1), U32, kind="Internal").ap()
    y_slots = nc.dram_tensor("y_slots", (TILES * P, D), F32, kind="Internal").ap()
    with ExitStack() as ctx:
        st = Stage(nc, ctx, name)
        wr = st.sb("wr", [P, NC, E])
        wgu = st.sb("wgu", [P, E, NC, 2 * HID])
        wd = st.sb("wd", [P, E, 3, D])
        slot = st.sb("slot", [P, T, PICKS], U32)
        share = st.sb("share", [P, T, PICKS])
        tile_expert = st.sb("tile_expert", [P, TILES], mybir.dt.int32)
        weights_loaded = st.sem("weights_loaded")

        with ExitStack() as ctx_r:
            sr = Stage(nc, ctx_r, name + "R")
            x_rows = x_in.rearrange("(b t p) d -> b p t d", p=P, t=NT)
            x = [sr.sb(f"x{p}", [P, NT, D]) for p in range(2)]
            xT = [sr.sb(f"xT{p}", [P, NC, S]) for p in range(2)]
            turn_ps = [sr.ps(f"turn_ps{p}", [P, 2, 512]) for p in range(2)]
            logit_ps = [sr.ps(f"logit_ps{p}", [P, 512]) for p in range(2)]
            count_ps = sr.ps("count_ps", [P, 2, T, E])
            lg, ranked, pos, m = (sr.sb(n, [P, T, E]) for n in ("lg", "ranked", "pos", "m"))
            ind = [sr.sb(f"ind{n}", [P, T, E]) for n in range(PICKS)]
            top = [sr.sb(f"top{n}", [P, T]) for n in range(PICKS)]
            which, diffs, den = (sr.sb(n, [P, T]) for n in ("which", "diffs", "den"))
            slot_f = sr.sb("slot_f", [P, T, PICKS])
            before = sr.sb("before", [P, T + 1, E])
            desc = sr.sb("desc", [P, E])
            levels = sr.sb("levels", [P, T])
            need = sr.sb("need", [P, E, T])
            tiles_of = sr.sb("tiles_of", [P, E])
            first_tile = sr.sb("first_tile", [P, E + 1])
            numbers = sr.sb("numbers", [P, TILES])
            past = sr.sb("past", [P, TILES, E])
            owner = sr.sb("owner", [P, TILES])
            earlier = sr.sb("earlier", [P, P])
            ones = sr.sb("ones", [P, P])
            ids = sr.sb("ids", [P, T], U32)
            zeros = sr.sb("zeros", [TILES, P], U32)
            x_loaded = [sr.sem(f"x_loaded{p}") for p in range(2)]
            sem = {n: sr.sem(n) for n in (
                "made", "shaped", "zeroed", "x_turned", "x_taken", "logits_ready", "logits_taken", "diff_ready",
                "exp_ready", "picks_ready", "counted", "slots_ready", "placed", "linked")}

            def lagged(eng, first, second):
                first(0, 0, 0)
                with eng.Fori(0, B // 2 - 1) as i:
                    first(2 * i + 1, i, 1)
                    second(2 * i, i, 0)
                    first(2 * i + 2, i + 1, 0)
                    second(2 * i + 1, i, 1)
                first(B - 1, B // 2 - 1, 1)
                second(B - 2, B // 2 - 1, 0)
                second(B - 1, B // 2 - 1, 1)

            with nc.Block() as block:
                @block.sync
                def _(sp):
                    sp.dma_start(wr[:], w_router.rearrange("(c p) e -> p c e", p=P)).then_inc(weights_loaded, 16)
                    for p in range(2):
                        sp.dma_start(x[p][:], x_rows[p]).then_inc(x_loaded[p], 16)
                    sp.wait_ge(sem["made"], 1)
                    sp.dma_start(token_of.rearrange("(a p) o -> a (p o)", p=P), zeros[:]).then_inc(sem["zeroed"], 16)
                    with sp.Fori(0, B // 2 - 1) as i:
                        for p in range(2):
                            sp.wait_ge(sem["x_turned"], 2 * i + p + 1)
                            sp.dma_start(x[p][:], x_rows[2 * i + p + 2]).then_inc(x_loaded[p], 16)
                    for e in range(E):
                        sp.dma_start(wgu[:, e], w_gu[e].rearrange("(c p) n -> p c n", p=P)).then_inc(weights_loaded, 16)
                        sp.dma_start(wd[:, e, 0:2, :], w_down[e, 0:2 * P].rearrange("(c p) n -> p c n", p=P)).then_inc(weights_loaded, 16)
                        sp.dma_start(wd[0:HID - 2 * P, e, 2, :], w_down[e, 2 * P:HID]).then_inc(weights_loaded, 16)

                @block.gpsimd
                def _(pool):
                    pool.memset(zeros[:], 0).then_inc(sem["made"], 1)
                    exact = {"allow_small_or_imprecise_dtypes": True}
                    pool.iota(desc[:], [[-1, E]], base=E, channel_multiplier=0, **exact).then_inc(sem["made"], 1)
                    pool.iota(levels[:], [[P, T]], base=0, channel_multiplier=0, **exact).then_inc(sem["made"], 1)
                    pool.iota(numbers[:], [[1, TILES]], base=0, channel_multiplier=0, **exact).then_inc(sem["made"], 1)
                    pool.iota(ids[:], [[P, T]], base=0, channel_multiplier=1).then_inc(sem["made"], 1)
                    pool.memset(earlier[:], 1.0).then_inc(sem["made"], 1)
                    pool.memset(ones[:], 1.0).then_inc(sem["made"], 1)
                    pool.wait_ge(sem["made"], 7)
                    pool.affine_select(out=earlier[:], in_=earlier[:], compare_op=ALU.is_gt, fill=0.0, base=0,
                                       pattern=[[1, P]], channel_multiplier=-1).then_inc(sem["shaped"], 1)
                    pool.wait_ge(sem["zeroed"], 16)
                    pool.wait_ge(sem["slots_ready"], 1)
                    for t in range(T):
                        for n in range(PICKS):
                            pool.indirect_dma_start(
                                out=token_of, out_offset=bass.IndirectOffsetOnAxis(ap=slot[:, t, n:n + 1], axis=0),
                                in_=ids[:, t:t + 1], in_offset=None).then_inc(sem["placed"], 16)
                    pool.wait_ge(sem["placed"], 16 * T * PICKS)

                @block.tensor
                def _(pe):
                    pe.wait_ge(weights_loaded, 16)

                    def turn(b, k, p):
                        pe.wait_ge(x_loaded[p], 16 * k + 16)
                        transpose_rows(pe, consts["ident"], turn_ps[p], x[p]).then_inc(sem["x_turned"], 1)

                    def logits(b, k, p):
                        pe.wait_ge(sem["x_taken"], b + 1)
                        if not (isinstance(b, int) and b == 0):
                            pe.wait_ge(sem["logits_taken"], b + 1)
                        for t in range(NT):
                            ins = project_rows(pe, logit_ps[p][:, t * E:(t + 1) * E], xT[p], t, wr, 0, E)
                        ins.then_inc(sem["logits_ready"], 1)
                    lagged(pe, turn, logits)

                    pe.wait_ge(sem["shaped"], 1)
                    pe.wait_ge(sem["picks_ready"], 1)
                    for n, mat in enumerate((earlier, ones)):
                        ins = pe.matmul(count_ps[:, n].rearrange("p t e -> p (t e)"), mat[:], m[:].rearrange("p t e -> p (t e)"),
                                        start=True, stop=True)
                    ins.then_inc(sem["counted"], 1)

                @block.scalar
                def _(act):
                    def batch(i, p):
                        act.wait_ge(sem["x_turned"], 2 * i + p + 1)
                        act.copy(xT[p][:].rearrange("p (a c) s -> p a (c s)", a=2), turn_ps[p][:]).then_inc(sem["x_taken"], 1)
                    batches(act, batch)
                    act.wait_ge(sem["diff_ready"], 1)
                    act.activation(share[:, :, 1], diffs[:], ACT.Exp).then_inc(sem["exp_ready"], 1)

                @block.vector
                def _(dve):
                    link = Link(dve, sem["linked"], 1 << 30)
                    dve.sem_inc(sem["logits_taken"], 1)

                    def batch(i, p):
                        dve.wait_ge(sem["logits_ready"], 2 * i + p + 1)
                        dve.tensor_copy(lg[:, bass.ds((2 * i + p) * NT, NT), :],
                                        logit_ps[p][:, 0:NT * E].rearrange("p (t e) -> p t e", e=E)).then_inc(sem["logits_taken"], 1)
                    batches(dve, batch)
                    dve.wait_ge(sem["logits_taken"], B + 1)
                    dve.wait_ge(sem["made"], 7)

                    def per_tile(a):
                        return a.unsqueeze(2).to_broadcast([P, T, E])

                    def per_expert(a):
                        return a.unsqueeze(1).to_broadcast([P, T, E])

                    for n in range(PICKS):
                        link.after(dve.tensor_reduce(top[n][:], lg[:], AX_X, ALU.max))
                        link.after(dve.tensor_tensor(ranked[:], lg[:], per_tile(top[n][:]), ALU.is_equal))
                        link.after(dve.tensor_tensor(ranked[:], ranked[:], per_expert(desc[:]), ALU.mult))
                        link.after(dve.tensor_reduce(which[:], ranked[:], AX_X, ALU.max))
                        link.after(dve.tensor_tensor(ind[n][:], ranked[:], per_tile(which[:]), ALU.is_equal))
                        if n == 0:
                            link.after(dve.scalar_tensor_tensor(out=lg[:], in0=ind[0][:], scalar=NEVER, in1=lg[:],
                                                                op0=ALU.mult, op1=ALU.add))
                    dve.tensor_tensor(m[:], ind[0][:], ind[1][:], ALU.add).then_inc(sem["picks_ready"], 1)
                    dve.tensor_tensor(diffs[:], top[1][:], top[0][:], ALU.subtract).then_inc(sem["diff_ready"], 1)
                    dve.wait_ge(sem["exp_ready"], 1)
                    link.after(dve.tensor_scalar(den[:], share[:, :, 1], 1.0, None, ALU.add))
                    link.after(dve.reciprocal(share[:, :, 0], den[:]))
                    link.after(dve.tensor_tensor(share[:, :, 1], share[:, :, 1], share[:, :, 0], ALU.mult))
                    link.after(dve.memset(before[:, 0, :], 0.0))
                    dve.wait_ge(sem["counted"], 1)
                    for t in range(T):
                        link.after(dve.tensor_tensor(before[:, t + 1, :], before[:, t, :], count_ps[:, 1, t, :], ALU.add))
                    link.after(dve.tensor_tensor(need[:], before[:, T, :].unsqueeze(2).to_broadcast([P, E, T]),
                                                 levels[:].unsqueeze(1).to_broadcast([P, E, T]), ALU.is_gt))
                    link.after(dve.tensor_reduce(tiles_of[:], need[:], AX_X, ALU.add))
                    link.after(dve.memset(first_tile[:, 0:1], 0.0))
                    for e in range(E):
                        link.after(dve.tensor_tensor(first_tile[:, e + 1:e + 2], first_tile[:, e:e + 1], tiles_of[:, e:e + 1], ALU.add))
                    link.after(dve.tensor_tensor(past[:], numbers[:].unsqueeze(2).to_broadcast([P, TILES, E]),
                                                 first_tile[:, 1:E + 1].unsqueeze(1).to_broadcast([P, TILES, E]), ALU.is_ge))
                    link.after(dve.tensor_reduce(owner[:], past[:], AX_X, ALU.add))
                    link.after(dve.tensor_scalar(owner[:], owner[:], float(E - 1), None, ALU.min))
                    link.after(dve.tensor_copy(tile_expert[:], owner[:]))
                    link.after(dve.tensor_tensor(pos[:], before[:, 0:T, :], count_ps[:, 0], ALU.add))
                    link.after(dve.scalar_tensor_tensor(out=pos[:], in0=per_expert(first_tile[:, 0:E]), scalar=float(P), in1=pos[:],
                                                        op0=ALU.mult, op1=ALU.add))
                    for n in range(PICKS):
                        link.after(dve.tensor_tensor(ranked[:], ind[n][:], pos[:], ALU.mult))
                        link.after(dve.tensor_reduce(slot_f[:, :, n], ranked[:], AX_X, ALU.add))
                    dve.tensor_copy(slot[:], slot_f[:]).then_inc(sem["slots_ready"], 1)

        with ExitStack() as ctx_m:
            sm = Stage(nc, ctx_m, name + "M")
            tokens = [sm.sb(f"tokens{p}", [P, 1], U32) for p in range(2)]
            xg = [sm.sb(f"xg{p}", [P, D]) for p in range(2)]
            xT = sm.sb("xT", [P, NC, P])
            silu = sm.sb("silu", [P, 2, HID])
            hid = sm.sb("hid", [P, 2, HID])
            hT = sm.sb("hT", [P, 3, P])
            y = [sm.sb(f"y{p}", [P, D]) for p in range(2)]
            gu_ps = sm.ps("gu_ps", [P, 2, 2, 512])
            xT_ps = sm.ps("xT_ps", [P, 512])
            hT_ps = sm.ps("hT_ps", [P, 512])
            y_ps = sm.ps("y_ps", [P, 2, 512])
            tokens_loaded = [sm.sem(f"tokens_loaded{p}") for p in range(2)]
            gathered = [sm.sem(f"gathered{p}") for p in range(2)]
            y_stored = [sm.sem(f"y_stored{p}") for p in range(2)]
            sem = {n: sm.sem(n) for n in (
                "x_turned", "xT_taken", "gu_ready", "silu_ready", "hid_ready", "h_turned", "hT_taken", "y_ready", "y_taken",
                "carried")}
            HALF = TILES // 2

            def tiles(eng, step):
                for p in range(2):
                    step(p, 0, p, True, None)
                with eng.Fori(1, HALF - 1) as i:
                    for p in range(2):
                        step(2 * i + p, i, p, False, None)
                for p in range(2):
                    step(TILES - 2 + p, HALF - 1, p, False, p)

            with nc.Block() as block:
                @block.sync
                def _(sp):
                    def load(s, p):
                        sp.dma_start(tokens[p][:], token_of[bass.ds(s * P, P), :]).then_inc(tokens_loaded[p], 16)

                    def step(s, k, p, first, last):
                        if last is None:
                            sp.wait_ge(gathered[p], 16 * k + 16)
                            load(s + 2, p)
                    for p in range(2):
                        load(p, p)
                    tiles(sp, step)

                @block.gpsimd
                def _(pool):
                    def step(s, k, p, first, last):
                        pool.wait_ge(tokens_loaded[p], 16 * k + 16)
                        if not first:
                            pool.wait_ge(sem["x_turned"], s - 1)
                        pool.sem_inc(sem["carried"], 1)
                        pool.indirect_dma_start(out=xg[p][:], out_offset=None, in_=x_in,
                                                in_offset=bass.IndirectOffsetOnAxis(ap=tokens[p][:], axis=0)).then_inc(gathered[p], 16)
                    tiles(pool, step)

                @block.tensor
                def _(pe):
                    pe.wait_ge(weights_loaded, 16 * (1 + 3 * E))

                    def expert(s):
                        return pe.value_load(tile_expert[0:1, bass.ds(s, 1)], min_val=0, max_val=E - 1)

                    def turn_x(s, k, p):
                        pe.wait_ge(gathered[p], 16 * k + 16)
                        if not (isinstance(s, int) and s == 0):
                            pe.wait_ge(sem["xT_taken"], s)
                        for c in range(NC):
                            ins = pe.transpose(xT_ps[:, c * P:(c + 1) * P], xg[p][:, c * P:(c + 1) * P], consts["ident"][:])
                        ins.then_inc(sem["x_turned"], 1)

                    def gate_up(s, p, first):
                        e = expert(s)
                        pe.wait_ge(sem["xT_taken"], s + 1)
                        if not first:
                            pe.wait_ge(sem["hid_ready"], s - 1)
                        for h in range(2):
                            for c in range(NC):
                                ins = pe.matmul(gu_ps[:, p, h, 0:HID], xT[:, c, :], wgu[:, e, c, h * HID:(h + 1) * HID],
                                                start=c == 0, stop=c == NC - 1)
                        ins.then_inc(sem["gu_ready"], 1)

                    def step(s, k, p, first, last):
                        if last != 1:
                            gate_up(s + 1, 1 - p, first and p == 0)
                        pe.wait_ge(sem["hid_ready"], s + 1)
                        if not (first and p == 0):
                            pe.wait_ge(sem["hT_taken"], s)
                        for n, (lo, w) in enumerate(HC):
                            ins = pe.transpose(hT_ps[0:w, n * P:(n + 1) * P], hid[:, p, lo:lo + w], consts["ident"][:])
                        ins.then_inc(sem["h_turned"], 1)
                        if last is None:
                            turn_x(s + 2, k + 1, p)
                        e = expert(s)
                        pe.wait_ge(sem["hT_taken"], s + 1)
                        if not first:
                            pe.wait_ge(sem["y_taken"], s - 1)
                        for n, (lo, w) in enumerate(HC):
                            ins = pe.matmul(y_ps[:, p, :], hT[0:w, n, :], wd[0:w, e, n, :], start=n == 0, stop=n == 2)
                        ins.then_inc(sem["y_ready"], 1)

                    turn_x(0, 0, 0)
                    gate_up(0, 0, True)
                    turn_x(1, 0, 1)
                    tiles(pe, step)

                @block.scalar
                def _(act):
                    def swish(s, p):
                        act.wait_ge(sem["gu_ready"], s + 1)
                        act.activation(silu[:, p, :], gu_ps[:, p, 0, 0:HID], ACT.Silu).then_inc(sem["silu_ready"], 1)

                    def step(s, k, p, first, last):
                        if last != 1:
                            swish(s + 1, 1 - p)
                        act.wait_ge(sem["h_turned"], s + 1)
                        act.copy(hT[:, 0:2, :], hT_ps[:, 0:2 * P].rearrange("p (k n) -> p k n", n=P))
                        w = HC[2][1]
                        act.copy(hT[0:w, 2, :], hT_ps[0:w, 2 * P:3 * P]).then_inc(sem["hT_taken"], 1)
                        if not (first and p == 0):
                            store(s - 1, 1 - p)
                    def store(s, p):
                        act.wait_ge(sem["y_taken"], s + 1)
                        act.dma_start(y_slots[bass.ds(s * P, P), :], y[p][:]).then_inc(y_stored[p], 16)
                    swish(0, 0)
                    tiles(act, step)
                    store(TILES - 1, (TILES - 1) % 2)
                    for p in range(2):
                        act.wait_ge(y_stored[p], 16 * HALF)

                @block.vector
                def _(dve):
                    def take_x(s):
                        dve.wait_ge(sem["x_turned"], s + 1)
                        dve.tensor_copy(xT[:], xT_ps[:].rearrange("p (c n) -> p c n", n=P)).then_inc(sem["xT_taken"], 1)

                    def product(s, p):
                        dve.wait_ge(sem["silu_ready"], s + 1)
                        dve.tensor_tensor(hid[:, p, :], gu_ps[:, p, 1, 0:HID], silu[:, p, :], ALU.mult).then_inc(sem["hid_ready"], 1)

                    def step(s, k, p, first, last):
                        if last != 1:
                            product(s + 1, 1 - p)
                        if last is None:
                            take_x(s + 2)
                        dve.wait_ge(sem["y_ready"], s + 1)
                        if not first:
                            dve.wait_ge(y_stored[p], 16 * k)
                        dve.tensor_copy(y[p][:], y_ps[:, p, :]).then_inc(sem["y_taken"], 1)
                    take_x(0)
                    product(0, 0)
                    take_x(1)
                    tiles(dve, step)

        with ExitStack() as ctx_f:
            sf = Stage(nc, ctx_f, name + "F")
            fr = Frame(sf, x_in, x_out)
            picked = [[sf.sb(f"picked{p}{n}", [P, NT, D]) for n in range(PICKS)] for p in range(2)]
            rows = [sf.sb(f"rows{p}", [P, NT, PICKS], U32) for p in range(2)]
            part = sf.sb("part", [P, NT, D])
            rows_ready, carried = sf.sem("rows_ready"), sf.sem("carried")
            fetched = [sf.sem(f"fetched{p}") for p in range(2)]
            linked = sf.sem("linked")
            with nc.Block() as block:
                @block.sync
                def _(sp):
                    fr.traffic(sp)

                @block.gpsimd
                def _(pool):
                    def fetch(b, p, first):
                        if not first:
                            pool.wait_ge(fr.summed, b)
                        pool.tensor_copy(rows[p][:], slot[:, bass.ds(b * NT, NT), :]).then_inc(rows_ready, 1)
                        pool.wait_ge(rows_ready, b + 1)
                        pool.sem_inc(carried, 1)
                        for t in range(NT):
                            for n in range(PICKS):
                                pool.indirect_dma_start(
                                    out=picked[p][n][:, t, :], out_offset=None, in_=y_slots,
                                    in_offset=bass.IndirectOffsetOnAxis(ap=rows[p][:, t, n:n + 1], axis=0)).then_inc(fetched[p], 16)
                    for p in range(2):
                        fetch(p, p, True)
                    with pool.Fori(0, B // 2 - 1) as i:
                        for p in range(2):
                            fr.root(pool, consts["minus_half"], 2 * i + p)
                            fetch(2 * i + p + 2, p, False)
                    for p in range(2):
                        fr.root(pool, consts["minus_half"], B - 2 + p)

                @block.vector
                def _(dve):
                    link = Link(dve, linked, Frame.LINKS + 1)

                    def batch(i, p):
                        b = 2 * i + p
                        link.start(b)
                        dve.wait_ge(fr.x_loaded[p], 16 * i + 16)
                        dve.wait_ge(fetched[p], 16 * NT * PICKS * (i + 1))
                        for t in range(NT):
                            ins = dve.scalar_tensor_tensor(out=part[:, t, :], in0=picked[p][0][:, t, :],
                                                           scalar=share[:, bass.ds(b * NT + t, 1), 0],
                                                           in1=fr.x[p][:, t, :], op0=ALU.mult, op1=ALU.add)
                        link.after(ins)
                        for t in range(NT):
                            ins = dve.scalar_tensor_tensor(out=fr.total[:, t, :], in0=picked[p][1][:, t, :],
                                                           scalar=share[:, bass.ds(b * NT + t, 1), 1],
                                                           in1=part[:, t, :], op0=ALU.mult, op1=ALU.add)
                        ins.then_inc(fr.summed, 1)
                        dve.wait_ge(fr.summed, b + 2)
                        fr.statistics(dve, link)
                        fr.finish(dve, i, p)
                    batches(dve, batch)


def make_toeplitz(nc, filt, filt_pad, toeplitz):
    H = filt.shape[0]
    with ExitStack() as ctx:
        st = Stage(nc, ctx, "toep")
        kp = st.sb("kp", [H, P + D])
        padded, k_loaded, pad_stored = st.sem("padded"), st.sem("k_loaded"), st.sem("pad_stored")
        toep_stored = nc.alloc_semaphore("toep_stored")
        with nc.Block() as block:
            @block.gpsimd
            def _(pool):
                pool.memset(kp[:], 0.0).then_inc(padded, 1)

            @block.sync
            def _(sp):
                sp.wait_ge(padded, 1)
                sp.dma_start(kp[:, P:P + D], filt).then_inc(k_loaded, 16)
                sp.wait_ge(k_loaded, 16)
                sp.dma_start(filt_pad, kp[:]).then_inc(pad_stored, 16)
                sp.wait_ge(pad_stored, 16)
                rows_up = bass.AP(tensor=filt_pad.tensor, offset=filt_pad.offset + P,
                                  ap=[[P + D, H], [-1, P], [1, D]])
                sp.dma_start(toeplitz, rows_up).then_inc(toep_stored, 16)
    return toep_stored


def decoder_kernel(nc, a, out):
    x = [a["x"]] + [nc.dram_tensor(f"x_after_{k}", (B * S, D), F32, kind="Internal").ap() for k in range(5)] + [out]
    toeplitz = nc.dram_tensor("toeplitz", (32, P, D), F32, kind="Internal").ap()
    filt_pad = nc.dram_tensor("filt_pad", (32, P + D), F32, kind="Internal").ap()
    with ExitStack() as ctx:
        consts = make_constants(nc, ctx)
        toep_stored = make_toeplitz(nc, a["L0_xattn_k"], filt_pad, toeplitz)
        causal_heads_stage(nc, consts, "diff", x[0], x[1], {
            "wq": a["L0_attn_Wq"], "wk": a["L0_attn_Wk"], "wv": a["L0_attn_Wv"], "wo": a["L0_attn_Wo"],
            "lq1": a["L0_attn_lambda_q1"], "lk1": a["L0_attn_lambda_k1"], "lq2": a["L0_attn_lambda_q2"],
            "lk2": a["L0_attn_lambda_k2"]}, "diff", norm_w=a["L0_attn_ln_w"])
        long_conv_stage(nc, consts, "conv", x[1], x[2], a["ctx_2048"], toeplitz, toep_stored, a["fside_S2_0"])
        experts_stage(nc, consts, "moe", x[2], x[3], a["L0_ffn_router_w"], a["L0_ffn_gate_up_proj"], a["L0_ffn_down_proj"])
        causal_heads_stage(nc, consts, "plain", x[3], x[4], {
            "wq": a["wq"], "wk": a["wk"], "wv": a["wv"], "wo": a["L1_attn_w_o"]}, "plain")
        long_cross_stage(nc, consts, "cross", x[4], x[5], a["ctx_2048"], {
            "wq": a["L1_xattn_wq"], "wk": a["L1_xattn_wk"], "wv": a["L1_xattn_wv"], "wo": a["L1_xattn_wo"]})
        causal_heads_stage(nc, consts, "shared", x[5], x[6], {
            "wq": a["gq"], "wk": a["gk"], "wv": a["gv"], "wgate": a["L1_ffn_W_gate"]}, "shared")


_ROWS = ("x", "ctx_2048")
_PLAIN = ("fside_S2_0", "L0_attn_lambda_q1", "L0_attn_lambda_k1", "L0_attn_lambda_q2", "L0_attn_lambda_k2",
          "L0_attn_ln_w", "L0_xattn_k")
_TURNED = ("L0_attn_Wq", "L0_attn_Wk", "L0_attn_Wv", "L0_attn_Wo", "L0_ffn_gate_up_proj", "L0_ffn_down_proj",
           "L0_ffn_router_w", "L1_attn_w_qkv", "L1_attn_w_o", "L1_xattn_wq", "L1_xattn_wk", "L1_xattn_wv",
           "L1_xattn_wo", "L1_ffn_W_gate", "L1_ffn_W_qkv")


def kernel(**inputs):
    import numpy as _np
    import concourse.bacc as _bacc
    from concourse.bass_utils import run_bass_kernel_spmd as _run

    nc = _bacc.Bacc("TRN2", target_bir_lowering=False, num_devices=1)
    arrays, args = {}, {}
    for name in _ROWS + _PLAIN + _TURNED:
        a = _np.asarray(inputs[name])
        if name in _ROWS:
            a = a.reshape(B * S, D)
        elif name in _TURNED:
            a = _np.swapaxes(a, -1, -2)
        a = _np.ascontiguousarray(a)
        arrays[f"in_{name}"] = a
        args[name] = nc.dram_tensor(f"in_{name}", a.shape, mybir.dt.from_np(a.dtype), kind="ExternalInput").ap()
    for src, names in (("L1_attn_w_qkv", ("wq", "wk", "wv")), ("L1_ffn_W_qkv", ("gq", "gk", "gv"))):
        for n, name in enumerate(names):
            args[name] = args[src][:, n * D:(n + 1) * D]
    out = nc.dram_tensor("out_x", (B * S, D), F32, kind="ExternalOutput").ap()
    decoder_kernel(nc, args, out)
    r = _run(nc, [arrays], core_ids=[0])
    return r.results[0]["out_x"].reshape(B, S, D)
```
